# Optimizing a Trainium2 kernel written in Bass

```python
import numpy as np
import jax
import jax.numpy as jnp

def _softmax(x, axis=-1):
    return jax.nn.softmax(x, axis=axis)

def _gelu(x):
    return jax.nn.gelu(x, approximate=True)

def _silu(x):
    return jax.nn.silu(x)

def _sigmoid(x):
    return jax.nn.sigmoid(x)

def _layernorm(x, axis=-1, eps=1e-05):
    m = jnp.mean(x, axis=axis, keepdims=True)
    v = jnp.var(x, axis=axis, keepdims=True)
    return (x - m) / jnp.sqrt(v + eps)

def _scatter_add(tgt, idx, src, axis=0):
    return tgt.at[idx].add(src)

def _segment_sum(src, seg, n):
    return jax.ops.segment_sum(src, seg, n)
kernel_name = 'mk_seq_preln_d1_jaxref_r4_55715e'

def setup_inputs(seed: int=0):
    np.random.seed(seed)
    _w = jnp.asarray

    def _L0_attn_setup():
        import jax, jax.numpy as jnp
        import numpy as np
        from jax import lax
        L, B, T, C, F = (4, 4, 512, 256, 1024)
        EPS = 1e-05

        def layernorm(x, w, b):
            m = jnp.mean(x, axis=-1, keepdims=True)
            v = jnp.var(x, axis=-1, keepdims=True)
            return (x - m) * lax.rsqrt(v + EPS) * w + b

        def time_shift(x):
            return jnp.pad(x, ((0, 0), (1, 0), (0, 0)))[:, :-1]

        def wkv(time_decay, time_first, k, v):
            w = -jnp.exp(time_decay)
            u = time_first
            kt = jnp.swapaxes(k, 0, 1)
            vt = jnp.swapaxes(v, 0, 1)
            Bn, Cn = (k.shape[0], k.shape[2])
            init = (jnp.zeros((Bn, Cn), k.dtype), jnp.zeros((Bn, Cn), k.dtype), jnp.full((Bn, Cn), -1e+38, k.dtype))

            def step(carry, kv):
                aa, bb, pp = carry
                kk, vv = kv
                ww = u + kk
                qq = jnp.maximum(pp, ww)
                e1 = jnp.exp(pp - qq)
                e2 = jnp.exp(ww - qq)
                out = (e1 * aa + e2 * vv) / (e1 * bb + e2)
                ww2 = pp + w
                qq2 = jnp.maximum(ww2, kk)
                e1b = jnp.exp(ww2 - qq2)
                e2b = jnp.exp(kk - qq2)
                return ((e1b * aa + e2b * vv, e1b * bb + e2b, qq2), out)
            _, out = lax.scan(step, init, (kt, vt))
            return jnp.swapaxes(out, 0, 1)
        key = jax.random.key(seed)
        ks = jax.random.split(key, 16)
        s = 0.02
        d = {}
        d['x'] = jax.random.normal(ks[0], (B, T, C), jnp.float32)
        d['ln0_w'] = jnp.ones((C,), jnp.float32)
        d['ln0_b'] = jnp.zeros((C,), jnp.float32)
        d['ln1_w'] = jnp.ones((L, C), jnp.float32)
        d['ln1_b'] = jnp.zeros((L, C), jnp.float32)
        d['ln2_w'] = jnp.ones((L, C), jnp.float32)
        d['ln2_b'] = jnp.zeros((L, C), jnp.float32)
        d['time_decay'] = jax.random.normal(ks[1], (L, C), jnp.float32) * 0.5
        d['time_first'] = jax.random.normal(ks[2], (L, C), jnp.float32) * 0.5 + jnp.float32(np.log(0.3))
        d['tmk'] = jax.random.uniform(ks[3], (L, C), jnp.float32)
        d['tmv'] = jax.random.uniform(ks[4], (L, C), jnp.float32)
        d['tmr'] = jax.random.uniform(ks[5], (L, C), jnp.float32)
        d['Wk'] = jax.random.normal(ks[6], (L, C, C), jnp.float32) * s
        d['Wv'] = jax.random.normal(ks[7], (L, C, C), jnp.float32) * s
        d['Wr'] = jax.random.normal(ks[8], (L, C, C), jnp.float32) * s
        d['Wo'] = jax.random.normal(ks[9], (L, C, C), jnp.float32) * s
        d['cmk'] = jax.random.uniform(ks[10], (L, C), jnp.float32)
        d['cmr'] = jax.random.uniform(ks[11], (L, C), jnp.float32)
        d['Wck'] = jax.random.normal(ks[12], (L, F, C), jnp.float32) * s
        d['Wcv'] = jax.random.normal(ks[13], (L, C, F), jnp.float32) * s
        d['Wcr'] = jax.random.normal(ks[14], (L, C, C), jnp.float32) * s
        return d
    _L0_attn_in = _L0_attn_setup()

    def _L0_ffn_setup():
        import jax, jax.numpy as jnp
        import numpy as np
        DM, NEXPERTS, SETS, ESIZE = (256, 32, 4, 32)
        B, S = (2, 2048)
        key = jax.random.key(seed)
        ks = jax.random.split(key, 7)
        sc = 0.02
        return {'x': jax.random.normal(ks[0], (B, S, DM), jnp.float32), 'Wc': jax.random.normal(ks[1], (DM, NEXPERTS, SETS), jnp.float32) * sc, 'bc': jax.random.normal(ks[2], (NEXPERTS, SETS), jnp.float32) * sc, 'W1': jax.random.normal(ks[3], (NEXPERTS, SETS, DM, ESIZE), jnp.float32) * sc, 'b1': jax.random.normal(ks[4], (NEXPERTS, SETS, ESIZE), jnp.float32) * sc, 'W2': jax.random.normal(ks[5], (NEXPERTS, SETS, DM, ESIZE), jnp.float32) * sc, 'b2': jax.random.normal(ks[6], (NEXPERTS, SETS, DM), jnp.float32) * sc}
    _L0_ffn_in = _L0_ffn_setup()
    _d = {'L0_attn_x': _L0_attn_in['x'], 'L0_attn_ln0_w': _L0_attn_in['ln0_w'], 'L0_attn_ln0_b': _L0_attn_in['ln0_b'], 'L0_attn_ln1_w': _L0_attn_in['ln1_w'], 'L0_attn_ln1_b': _L0_attn_in['ln1_b'], 'L0_attn_ln2_w': _L0_attn_in['ln2_w'], 'L0_attn_ln2_b': _L0_attn_in['ln2_b'], 'L0_attn_time_decay': _L0_attn_in['time_decay'], 'L0_attn_time_first': _L0_attn_in['time_first'], 'L0_attn_tmk': _L0_attn_in['tmk'], 'L0_attn_tmv': _L0_attn_in['tmv'], 'L0_attn_tmr': _L0_attn_in['tmr'], 'L0_attn_Wk': _L0_attn_in['Wk'], 'L0_attn_Wv': _L0_attn_in['Wv'], 'L0_attn_Wr': _L0_attn_in['Wr'], 'L0_attn_Wo': _L0_attn_in['Wo'], 'L0_attn_cmk': _L0_attn_in['cmk'], 'L0_attn_cmr': _L0_attn_in['cmr'], 'L0_attn_Wck': _L0_attn_in['Wck'], 'L0_attn_Wcv': _L0_attn_in['Wcv'], 'L0_attn_Wcr': _L0_attn_in['Wcr'], 'L0_ffn_Wc': _L0_ffn_in['Wc'], 'L0_ffn_bc': _L0_ffn_in['bc'], 'L0_ffn_W1': _L0_ffn_in['W1'], 'L0_ffn_b1': _L0_ffn_in['b1'], 'L0_ffn_W2': _L0_ffn_in['W2'], 'L0_ffn_b2': _L0_ffn_in['b2']}
    _x0 = _d['L0_attn_x']
    _d['L0_attn_x'] = jax.random.normal(jax.random.fold_in(jax.random.key(seed), 1), (16, 512, 256), dtype=_x0.dtype)
    del _x0
    return _d

def reference(L0_attn_x, L0_attn_ln0_w, L0_attn_ln0_b, L0_attn_ln1_w, L0_attn_ln1_b, L0_attn_ln2_w, L0_attn_ln2_b, L0_attn_time_decay, L0_attn_time_first, L0_attn_tmk, L0_attn_tmv, L0_attn_tmr, L0_attn_Wk, L0_attn_Wv, L0_attn_Wr, L0_attn_Wo, L0_attn_cmk, L0_attn_cmr, L0_attn_Wck, L0_attn_Wcv, L0_attn_Wcr, L0_ffn_Wc, L0_ffn_bc, L0_ffn_W1, L0_ffn_b1, L0_ffn_W2, L0_ffn_b2):

    def _L0_attn_ref(x, ln0_w, ln0_b, ln1_w, ln1_b, ln2_w, ln2_b, time_decay, time_first, tmk, tmv, tmr, Wk, Wv, Wr, Wo, cmk, cmr, Wck, Wcv, Wcr):
        import jax, jax.numpy as jnp
        import numpy as np
        from jax import lax
        L, B, T, C, F = (4, 4, 512, 256, 1024)
        EPS = 1e-05

        def layernorm(x, w, b):
            m = jnp.mean(x, axis=-1, keepdims=True)
            v = jnp.var(x, axis=-1, keepdims=True)
            return (x - m) * lax.rsqrt(v + EPS) * w + b

        def time_shift(x):
            return jnp.pad(x, ((0, 0), (1, 0), (0, 0)))[:, :-1]

        def wkv(time_decay, time_first, k, v):
            w = -jnp.exp(time_decay)
            u = time_first
            kt = jnp.swapaxes(k, 0, 1)
            vt = jnp.swapaxes(v, 0, 1)
            Bn, Cn = (k.shape[0], k.shape[2])
            init = (jnp.zeros((Bn, Cn), k.dtype), jnp.zeros((Bn, Cn), k.dtype), jnp.full((Bn, Cn), -1e+38, k.dtype))

            def step(carry, kv):
                aa, bb, pp = carry
                kk, vv = kv
                ww = u + kk
                qq = jnp.maximum(pp, ww)
                e1 = jnp.exp(pp - qq)
                e2 = jnp.exp(ww - qq)
                out = (e1 * aa + e2 * vv) / (e1 * bb + e2)
                ww2 = pp + w
                qq2 = jnp.maximum(ww2, kk)
                e1b = jnp.exp(ww2 - qq2)
                e2b = jnp.exp(kk - qq2)
                return ((e1b * aa + e2b * vv, e1b * bb + e2b, qq2), out)
            _, out = lax.scan(step, init, (kt, vt))
            return jnp.swapaxes(out, 0, 1)
        x = layernorm(x, ln0_w, ln0_b)
        for l in range(L):
            h = layernorm(x, ln1_w[l], ln1_b[l])
            hh = time_shift(h)
            xk = h * tmk[l] + hh * (1 - tmk[l])
            xv = h * tmv[l] + hh * (1 - tmv[l])
            xr = h * tmr[l] + hh * (1 - tmr[l])
            k = jnp.einsum('btc,oc->bto', xk, Wk[l])
            v = jnp.einsum('btc,oc->bto', xv, Wv[l])
            sr = jax.nn.sigmoid(jnp.einsum('btc,oc->bto', xr, Wr[l]))
            rwkv = sr * wkv(time_decay[l], time_first[l], k, v)
            x = x + jnp.einsum('bto,co->btc', rwkv, Wo[l])
            h = layernorm(x, ln2_w[l], ln2_b[l])
            hh = time_shift(h)
            xk = h * cmk[l] + hh * (1 - cmk[l])
            xr = h * cmr[l] + hh * (1 - cmr[l])
            kf = jnp.einsum('btc,fc->btf', xk, Wck[l])
            kf = jnp.square(jax.nn.relu(kf))
            kv = jnp.einsum('btf,cf->btc', kf, Wcv[l])
            x = x + jax.nn.sigmoid(jnp.einsum('btc,oc->bto', xr, Wcr[l])) * kv
        return x

    def _L0_ffn_ref(x, Wc, bc, W1, b1, W2, b2):
        import jax, jax.numpy as jnp
        import numpy as np
        DM, NEXPERTS, SETS, ESIZE = (256, 32, 4, 32)
        B, S = (2, 2048)
        b, s, d = x.shape
        g = Wc.shape[1]
        grouped = x.reshape(b, s // g, g, d)
        logits = jnp.einsum('bntd,des->bntes', grouped, Wc) + bc
        tie = jnp.linspace(0.0, 1e-06, g, dtype=x.dtype).reshape(-1, 1, 1)
        logits = logits + tie
        perm = (logits == jnp.max(logits, axis=-3, keepdims=True)).astype(x.dtype)
        permuted = jnp.einsum('bntd,bntes->bnesd', grouped, perm)
        inner = jax.nn.relu(jnp.einsum('bnesd,esdf->bnesf', permuted, W1) + b1)
        result_permuted = jnp.einsum('bnesf,esdf->bnesd', inner, W2) + b2
        result = jnp.einsum('bnesd,bntes->bntd', result_permuted, perm)
        return result.reshape(b, s, d)
    x = L0_attn_x
    x = x + _L0_attn_ref(_layernorm(x, axis=-1), L0_attn_ln0_w, L0_attn_ln0_b, L0_attn_ln1_w, L0_attn_ln1_b, L0_attn_ln2_w, L0_attn_ln2_b, L0_attn_time_decay, L0_attn_time_first, L0_attn_tmk, L0_attn_tmv, L0_attn_tmr, L0_attn_Wk, L0_attn_Wv, L0_attn_Wr, L0_attn_Wo, L0_attn_cmk, L0_attn_cmr, L0_attn_Wck, L0_attn_Wcv, L0_attn_Wcr)
    x = x + _L0_ffn_ref(_layernorm(x, axis=-1), L0_ffn_Wc, L0_ffn_bc, L0_ffn_W1, L0_ffn_b1, L0_ffn_W2, L0_ffn_b2)
    return x

_drawn_inputs = setup_inputs


def setup_inputs(seed=0):
    import zlib

    import numpy as np

    out = dict(_drawn_inputs(seed))
    spreads = {'L0_attn_ln0_w': (1.0, 0.2),
     'L0_attn_ln0_b': (0.0, 0.1),
     'L0_attn_ln1_w': (1.0, 0.6),
     'L0_attn_ln1_b': (0.0, 0.8),
     'L0_attn_ln2_w': (1.0, 0.6),
     'L0_attn_ln2_b': (0.0, 0.8)}
    factors = {'L0_attn_time_decay': 7.362,
     'L0_attn_time_first': 8.0,
     'L0_attn_tmk': 8.0,
     'L0_attn_tmv': 5.827,
     'L0_attn_tmr': 8.0,
     'L0_attn_Wk': 8.0,
     'L0_attn_Wr': 8.0,
     'L0_attn_cmk': 3.485,
     'L0_attn_cmr': 8.0,
     'L0_attn_Wcr': 8.0,
     'L0_ffn_W1': 2.719,
     'L0_ffn_b1': 47.852,
     'L0_ffn_b2': 2.882}
    for name, (base, spread) in spreads.items():
        noise = np.random.default_rng([zlib.crc32(name.encode()), seed]).standard_normal(out[name].shape)
        drawn = base * np.exp(spread * noise) if base else spread * noise
        out[name] = jnp.asarray(drawn.astype(out[name].dtype))
    for name, factor in factors.items():
        out[name] = (out[name] * factor).astype(out[name].dtype)
    return out
```

```python
import concourse.bass as bass
from concourse import mybir
from contextlib import ExitStack

F32 = mybir.dt.float32
ALU = mybir.AluOpType
ACT = mybir.ActivationFunctionType
AX = mybir.AxisListType

P = 128
SEQS, T, C, F = 16, 512, 256, 1024
LAYERS = 4
CB, FB, TT = C // P, F // P, T // P
STEPS = LAYERS * SEQS
EPS = 1e-5
NEG = -1e38
(LN1W, LN1B, LN2W, LN2B, DECAY, FIRST, TMK, TMV, TMR, CMK, CMR) = range(11)
NPAR = 11

G = 32
E_, S_, EF = 32, 4, 32
ES = E_ * S_
CH = 2
CHUNKS = SEQS // CH
CTT = CH * TT
NG = CH * T // G


def rwkv_moe(nc, x_in, ln0, par_in, kvr_in, wo_in, wck_in, wcr_in, wcv_in, ident_in,
             wc_in, bctie_in, w1_in, b1_in, w2_in, b2_in, out):
    outer = ExitStack()
    with outer:
        x = outer.enter_context(nc.sbuf_tensor("x", [P, SEQS, TT, C], F32))
        ident = outer.enter_context(nc.sbuf_tensor("ident", [P, P], F32))
        eps_pow = outer.enter_context(nc.sbuf_tensor("eps_pow", [P, CTT], F32))
        first_norms(nc, x, ident, eps_pow, x_in, ln0, ident_in)
        layers(nc, x, ident, eps_pow, par_in, kvr_in, wo_in, wck_in, wcr_in, wcv_in)
        experts(nc, x, ident, eps_pow, x_in, wc_in, bctie_in, w1_in, b1_in, w2_in, b2_in, out)


def later(count):
    return not isinstance(count, int) or count > 0


def held(dve, spare, sem, count):
    dve.wait_ge(sem, count)
    dve.memset(spare, 0.0)


def first_norms(nc, x, ident, eps_pow, x_in, ln0, ident_in):
    ctx = ExitStack()
    with ctx:
        def sb(name, shape):
            return ctx.enter_context(nc.sbuf_tensor(name, shape, F32))

        def sem(name):
            return ctx.enter_context(nc.semaphore(name))

        ln0_sb = sb("ln0_sb", [P, 2, C])
        spare = sb("spare0", [P, 1])
        st = sb("st", [P, TT, 6])
        mv = sb("mv", [P, TT, 2])
        ve = sb("ve", [P, TT])
        rstd = sb("rstd", [P, TT])
        x_loaded = [sem("x_even_loaded"), sem("x_odd_loaded")]
        const_loaded, const_set = sem("const_loaded"), sem("const_set")
        stats_done, aggr_done, var_done, rstd_done, norm_done = (
            sem("stats_done"), sem("aggr_done"), sem("var_done"), sem("rstd_done"), sem("norm_done"))
        scaled = sem("scaled")
        block = ctx.enter_context(nc.Block())

        @block.sync
        def _(sp):
            sp.dma_start(ln0_sb[:], ln0.unsqueeze(0).to_broadcast([P, 2, C])).then_inc(const_loaded, 16)
            sp.dma_start(ident[:], ident_in).then_inc(const_loaded, 16)

            def load(s, odd):
                sp.dma_start(x[:, bass.ds(s, 1), :, :].rearrange("p s t c -> p (s t) c"),
                             x_in[bass.ds(s, 1)].rearrange("s (t p) c -> p (s t) c", p=P)).then_inc(x_loaded[odd], 16)

            load(0, 0)
            load(1, 1)
            with sp.Fori(1, SEQS // 2) as pair:
                for odd in range(2):
                    s = 2 * pair
                    sp.wait_ge(stats_done, 2 * (s + odd) - 3)
                    load(s + odd, odd)
            sp.wait_ge(const_loaded, 32)

        @block.gpsimd
        def _(pool):
            pool.memset(eps_pow[:], -0.5).then_inc(const_set, 1)
            pool.wait_ge(const_set, 1)
            with pool.Fori(0, 2 * SEQS) as n:
                pool.wait_ge(var_done, n + 1)
                pool.tensor_tensor(rstd[:], ve[:], eps_pow[:, 0:TT], ALU.pow).then_inc(rstd_done, 1)

        @block.vector
        def _(dve):
            dve.wait_ge(const_loaded, 32)
            with dve.Fori(0, SEQS // 2) as pair:
                for odd in range(2):
                    s = 2 * pair + odd
                    xs = x[:, bass.ds(s, 1), :, :].rearrange("p s t c -> p (s t) c")
                    held(dve, spare[:], x_loaded[odd], 16 * pair + 16)
                    for r in range(2):
                        if r:
                            held(dve, spare[:], norm_done, 2 * s + 1)
                        for t in range(TT):
                            last = dve.bn_stats(st[:, t, :], xs[:, t, :])
                        last.then_inc(stats_done, 1)
                        held(dve, spare[:], stats_done, 2 * s + r + 1)
                        for t in range(TT):
                            last = dve.bn_aggr(mv[:, t, :], st[:, t, :])
                        last.then_inc(aggr_done, 1)
                        dve.wait_ge(aggr_done, 2 * s + r + 1)
                        dve.tensor_scalar(ve[:], mv[:, :, 1], EPS, None, ALU.add).then_inc(var_done, 1)
                        dve.wait_ge(rstd_done, 2 * s + r + 1)
                        for t in range(TT):
                            last = dve.tensor_scalar(xs[:, t, :], xs[:, t, :], mv[:, t, 0:1], rstd[:, t:t + 1],
                                                     ALU.subtract, ALU.mult)
                        last.then_inc(norm_done, 1)
                    dve.wait_ge(norm_done, 2 * s + 2)
                    dve.tensor_tensor(xs, xs, ln0_sb[:, 0:1, :].to_broadcast([P, TT, C]), ALU.mult).then_inc(scaled, 1)
                    dve.wait_ge(scaled, s + 1)
                    dve.tensor_tensor(xs, xs, ln0_sb[:, 1:2, :].to_broadcast([P, TT, C]), ALU.add)


def layers(nc, x, ident, eps_pow, par_in, kvr_in, wo_in, wck_in, wcr_in, wcv_in):
    ctx = ExitStack()
    with ctx:
        def sb(name, shape):
            return ctx.enter_context(nc.sbuf_tensor(name, shape, F32))

        def sem(name):
            return ctx.enter_context(nc.semaphore(name))

        U = [P, CB, T]
        spare = sb("spare1", [P, 1])
        par = sb("par", [P, NPAR, LAYERS, CB])
        kvr_w = sb("kvr_w", [P, 3, CB, C])
        wo_w = sb("wo_w", [P, CB, C])
        wck_w = sb("wck_w", [P, CB, F])
        wcr_w = sb("wcr_w", [P, CB, C])
        wcv_w = sb("wcv_w", [P, FB, C])

        st = [sb(f"st{a}", [P, TT, 6]) for a in range(2)]
        mv = [sb(f"mv{a}", [P, TT, 2]) for a in range(2)]
        ve = [sb(f"ve{a}", [P, TT]) for a in range(2)]
        rstd = [sb(f"rstd{a}", [P, TT]) for a in range(2)]
        xd = [sb(f"xd{a}", U) for a in range(2)]
        h = [sb(f"h{a}", [P, CB, T + 1]) for a in range(2)]
        xk, xv, xr = sb("xk", U), sb("xv", U), sb("xr", U)
        xk2, xr2 = sb("xk2", U), sb("xr2", U)
        kf = sb("kf", [P, FB, T])
        th2 = sb("th2", [P, TT * C])
        k_sb, v_sb, th = sb("k_sb", U), sb("v_sb", U), sb("th", U)
        pp = sb("pp", [P, CB, T + 1])
        aa = sb("aa", [P, CB, T + 1])
        bb = sb("bb", [P, CB, T + 1])
        e1b, e2b = sb("e1b", U), sb("e2b", U)
        nd = sb("nd", U)
        e12 = sb("e12", [P, 2, CB, T])
        m1, rw = sb("m1", U), sb("rw", U)

        pairs = [ctx.enter_context(nc.psum_tensor(f"pair{a}", [P, 2, 512], F32)) for a in range(4)]

        par_loaded, par_exp, par_ready = sem("par_loaded"), sem("par_exp"), sem("par_ready")
        edges = sem("edges")
        kvr_loaded, wo_loaded, ck_loaded, cv_loaded = sem("kvr_loaded"), sem("wo_loaded"), sem("ck_loaded"), sem("cv_loaded")
        stats = [sem("stats1"), sem("stats2")]
        aggr = [sem("aggr1"), sem("aggr2")]
        var = [sem("var1"), sem("var2")]
        rs = [sem("rstd1_ready"), sem("rstd2_ready")]
        xn = [sem("xn1"), sem("xn2")]
        tr = [sem("tr1"), sem("tr2")]
        hs = [sem("h1_ready"), sem("h2_ready")]
        ds_ = [sem("d1_ready"), sem("d2_ready")]
        mixed1, mixed2 = sem("mixed1"), sem("mixed2")
        k_done, v_done, r_done = sem("k_done"), sem("v_done"), sem("r_done")
        k_copied, v_copied, th_ready = sem("k_copied"), sem("v_copied"), sem("th_ready")
        pp_ready, e1_arg, e2_arg = sem("pp_ready"), sem("e1_arg"), sem("e2_arg")
        nd_ready, e12_arg, e12_ready = sem("nd_ready"), sem("e12_arg"), sem("e12_ready")
        e1b_ready, e2b_ready, ev_ready = sem("e1b_ready"), sem("e2b_ready"), sem("ev_ready")
        states = sem("states")
        m1_ready, m2_ready, m3_ready = sem("m1_ready"), sem("m2_ready"), sem("m3_ready")
        num_ready, den_ready, ln_ready, rden_ready = sem("num_ready"), sem("den_ready"), sem("ln_ready"), sem("rden_ready")
        gated, rw_ready = sem("gated"), sem("rw_ready")
        wo_done, x_mid = sem("wo_done"), sem("x_mid")
        cr_done, th2_ready = sem("cr_done"), sem("th2_ready")
        ck_done, relu_done, kf_ready = sem("ck_done"), sem("relu_done"), sem("kf_ready")
        cv_done, gated2, x_done = sem("cv_done"), sem("gated2"), sem("x_done")
        block = ctx.enter_context(nc.Block())

        def pipeline(engine, step):
            step(0, True, False, True)
            step(1, True, True, True)
            with engine.Fori(2, STEPS - 1) as i:
                step(i, True, True, True)
            step(STEPS - 1, True, True, False)
            step(STEPS, False, True, False)

        def seq(n):
            return x[:, bass.ds(n % SEQS, 1), :, :].rearrange("p s t c -> p (s t) c")

        def col(which, n, cb):
            return par[:, which, bass.ds(n // SEQS, 1), cb]

        @block.sync
        def _(sp):
            sp.dma_start(par[:], par_in).then_inc(par_loaded, 16)

            def load(l):
                def layer(t):
                    return t[bass.ds(l, 1)].rearrange("l p n -> (l p) n")
                if later(SEQS * l):
                    sp.wait_ge(r_done, SEQS * l)
                sp.dma_start(kvr_w[:].rearrange("p a b c -> p (a b c)"), layer(kvr_in)).then_inc(kvr_loaded, 16)
                if later(SEQS * l):
                    sp.wait_ge(wo_done, SEQS * l)
                sp.dma_start(wo_w[:].rearrange("p b c -> p (b c)"), layer(wo_in)).then_inc(wo_loaded, 16)
                if later(4 * SEQS * l):
                    sp.wait_ge(ck_done, 4 * SEQS * l)
                sp.dma_start(wcr_w[:].rearrange("p b c -> p (b c)"), layer(wcr_in)).then_inc(ck_loaded, 16)
                sp.dma_start(wck_w[:].rearrange("p b c -> p (b c)"), layer(wck_in)).then_inc(ck_loaded, 16)
                if later(SEQS * l):
                    sp.wait_ge(cv_done, SEQS * l)
                sp.dma_start(wcv_w[:].rearrange("p b c -> p (b c)"), layer(wcv_in)).then_inc(cv_loaded, 16)

            load(0)
            with sp.Fori(1, LAYERS) as l:
                load(l)

        @block.tensor
        def _(pe):
            def channel_major(pair, w, inp, blocks, done):
                for j, m in enumerate(blocks):
                    for cb in range(CB):
                        last = pe.matmul(pair[:, j, :], w[:, cb, m * P:(m + 1) * P], inp[:, cb, :],
                                         start=cb == 0, stop=cb == CB - 1)
                last.then_inc(done, 1)

            def token_major(pair, inp, w, nb, done):
                for t in range(TT):
                    for b in range(nb):
                        last = pe.matmul(pair[:, t // 2, (t % 2) * C:(t % 2 + 1) * C], inp[:, b, t * P:(t + 1) * P],
                                         w[:, b, :], start=b == 0, stop=b == nb - 1)
                last.then_inc(done, 1)

            def transposes(pair, a, n):
                pe.wait_ge(xn[a], n + 1)
                xt = xd[a][:].rearrange("p a b -> p (a b)").rearrange("p (t c) -> p t c", t=TT)
                for cb in range(CB):
                    for t in range(TT):
                        last = pe.transpose(pair[:, cb, t * P:(t + 1) * P], xt[:, t, cb * P:(cb + 1) * P], ident[:])
                last.then_inc(tr[a], 1)

            def step(i, now, prev, nxt):
                m = i - 1
                if now:
                    pe.wait_ge(kvr_loaded, 16 * (i // SEQS) + 16)
                    if prev:
                        if later(4 * m):
                            pe.wait_ge(relu_done, 4 * m)
                        if later(i):
                            pe.wait_ge(k_copied, i)
                    pe.wait_ge(mixed1, 3 * i + 1)
                    channel_major(pairs[0], kvr_w[:, 0], xk, range(CB), k_done)
                    pe.wait_ge(mixed1, 3 * i + 2)
                    channel_major(pairs[1], kvr_w[:, 1], xv, range(CB), v_done)
                    if prev:
                        if later(m):
                            pe.wait_ge(x_done, m)
                        if later(i):
                            pe.wait_ge(th_ready, i)
                    pe.wait_ge(mixed1, 3 * i + 3)
                    channel_major(pairs[2], kvr_w[:, 2], xr, range(CB), r_done)
                if prev:
                    transposes(pairs[3], 1, m)
                    if now:
                        pe.wait_ge(k_copied, i + 1)
                    else:
                        if later(4 * m):
                            pe.wait_ge(relu_done, 4 * m)
                    pe.wait_ge(ck_loaded, 32 * (m // SEQS) + 32)
                    pe.wait_ge(mixed2, 2 * m + 1)
                    token_major(pairs[0], xr2, wcr_w, CB, cr_done)
                    pe.wait_ge(mixed2, 2 * m + 2)
                    if now:
                        pe.wait_ge(v_copied, i + 1)
                    channel_major(pairs[1], wck_w, xk2, (0, 1), ck_done)
                    if now:
                        pe.wait_ge(th_ready, i + 1)
                    else:
                        if later(m):
                            pe.wait_ge(x_done, m)
                    channel_major(pairs[2], wck_w, xk2, (2, 3), ck_done)
                    channel_major(pairs[3], wck_w, xk2, (4, 5), ck_done)
                    pe.wait_ge(th2_ready, m + 1)
                    channel_major(pairs[0], wck_w, xk2, (6, 7), ck_done)
                if nxt:
                    if prev:
                        pe.wait_ge(relu_done, 4 * m + 1)
                    elif now:
                        pe.wait_ge(v_copied, i + 1)
                    transposes(pairs[1], 0, i + 1)
                if prev:
                    pe.wait_ge(cv_loaded, 16 * (m // SEQS) + 16)
                    pe.wait_ge(kf_ready, 4 * m + 4)
                    token_major(pairs[2], kf, wcv_w, FB, cv_done)
                if now:
                    pe.wait_ge(wo_loaded, 16 * (i // SEQS) + 16)
                    pe.wait_ge(rw_ready, i + 1)
                    token_major(pairs[3], rw, wo_w, CB, wo_done)

            transposes(pairs[1], 0, 0)
            pipeline(pe, step)

        @block.scalar
        def _(act):
            def affine(pair, a, n, ready):
                act.wait_ge(tr[a], n + 1)
                if a:
                    if later(2 * n):
                        act.wait_ge(mixed2, 2 * n)
                else:
                    if later(3 * n):
                        act.wait_ge(mixed1, 3 * n)
                wi, bi = (LN2W, LN2B) if a else (LN1W, LN1B)
                for cb in range(CB):
                    last = act.activation(h[a][:, cb, 1:], pair[:, cb, :], ACT.Identity,
                                          bias=col(bi, n, cb), scale=col(wi, n, cb))
                last.then_inc(ready, 1)

            def relu(m, j):
                act.wait_ge(ck_done, 4 * m + j + 1)
                if not j:
                    if later(m):
                        act.wait_ge(cv_done, m)
                act.activation(kf[:, 2 * j:2 * j + 2, :], pairs[(j + 1) % 4][:], ACT.Relu).then_inc(relu_done, 1)

            def step(i, now, prev, nxt):
                m = i - 1
                if now:
                    act.wait_ge(k_done, i + 1)
                    if prev:
                        if later(i):
                            act.wait_ge(rw_ready, i)
                    act.activation(k_sb[:], pairs[0][:], ACT.Identity).then_inc(k_copied, 1)
                    act.wait_ge(v_done, i + 1)
                    act.activation(v_sb[:], pairs[1][:], ACT.Identity).then_inc(v_copied, 1)
                if prev:
                    affine(pairs[3], 1, m, hs[1])
                if now:
                    act.wait_ge(r_done, i + 1)
                    act.activation(th[:], pairs[2][:], ACT.Tanh, scale=0.5).then_inc(th_ready, 1)
                if prev:
                    act.wait_ge(cr_done, m + 1)
                    if later(m):
                        act.wait_ge(x_done, m)
                    act.activation(th2[:], pairs[0][:].rearrange("p a b -> p (a b)"), ACT.Tanh, scale=0.5)\
                       .then_inc(th2_ready, 1)
                if now:
                    act.wait_ge(e1_arg, i + 1)
                    for cb in range(CB):
                        last = act.activation(e1b[:, cb, :], e1b[:, cb, :], ACT.Exp, bias=col(DECAY, i, cb))
                    last.then_inc(e1b_ready, 1)
                    act.wait_ge(e2_arg, i + 1)
                    act.activation(e2b[:], e2b[:], ACT.Exp).then_inc(e2b_ready, 1)
                if prev:
                    relu(m, 0)
                if now:
                    act.wait_ge(e12_arg, 2 * i + 2)
                    act.activation(e12[:], e12[:], ACT.Exp).then_inc(e12_ready, 1)
                if prev:
                    relu(m, 1)
                    relu(m, 2)
                    relu(m, 3)
                if now:
                    act.wait_ge(den_ready, i + 1)
                    den = e12[:, 0]
                    act.activation(den, den, ACT.Ln).then_inc(ln_ready, 1)
                    act.wait_ge(ln_ready, i + 1)
                    act.activation(den, den, ACT.Exp, scale=-1.0).then_inc(rden_ready, 1)
                if nxt:
                    affine(pairs[1], 0, i + 1, hs[0])

            act.wait_ge(par_loaded, 16)
            act.activation(par[:, DECAY], par[:, DECAY], ACT.Exp).then_inc(par_exp, 1)
            act.wait_ge(par_ready, 1)
            act.wait_ge(edges, 5)
            affine(pairs[1], 0, 0, hs[0])
            pipeline(act, step)

        @block.gpsimd
        def _(pool):
            def power(a, n):
                pool.wait_ge(var[a], n + 1)
                pool.tensor_tensor(rstd[a][:], ve[a][:], eps_pow[:, 0:TT], ALU.pow).then_inc(rs[a], 1)

            def diff(a, n):
                pool.wait_ge(hs[a], n + 1)
                pool.tensor_tensor(xd[a][:], h[a][:, :, 1:], h[a][:, :, 0:T], ALU.subtract).then_inc(ds_[a], 1)

            def step(i, now, prev, nxt):
                m = i - 1
                if prev:
                    power(1, m)
                if now:
                    pool.wait_ge(pp_ready, i + 1)
                    pool.tensor_tensor(e1b[:], pp[:, :, 0:T], pp[:, :, 1:], ALU.subtract).then_inc(e1_arg, 1)
                if prev:
                    diff(1, m)
                    for j in range(4):
                        pool.wait_ge(relu_done, 4 * m + j + 1)
                        pool.tensor_tensor(kf[:, 2 * j:2 * j + 2, :], kf[:, 2 * j:2 * j + 2, :],
                                           kf[:, 2 * j:2 * j + 2, :], ALU.mult).then_inc(kf_ready, 1)
                if nxt:
                    power(0, i + 1)
                    diff(0, i + 1)

            power(0, 0)
            diff(0, 0)
            pipeline(pool, step)

        @block.vector
        def _(dve):
            def norm_stats(a, n):
                xs = seq(n)
                for t in range(TT):
                    last = dve.bn_stats(st[a][:, t, :], xs[:, t, :])
                last.then_inc(stats[a], 1)
                held(dve, spare[:], stats[a], n + 1)
                for t in range(TT):
                    last = dve.bn_aggr(mv[a][:, t, :], st[a][:, t, :])
                last.then_inc(aggr[a], 1)
                dve.wait_ge(aggr[a], n + 1)
                dve.tensor_scalar(ve[a][:], mv[a][:, :, 1], EPS, None, ALU.add).then_inc(var[a], 1)

            def normalise(a, n):
                xs = seq(n)
                xt = xd[a][:].rearrange("p a b -> p (a b)").rearrange("p (t c) -> p t c", t=TT)
                dve.wait_ge(rs[a], n + 1)
                for t in range(TT):
                    last = dve.tensor_scalar(xt[:, t, :], xs[:, t, :], mv[a][:, t, 0:1], rstd[a][:, t:t + 1],
                                             ALU.subtract, ALU.mult)
                last.then_inc(xn[a], 1)

            def mix(dst, a, which, n, ready):
                for cb in range(CB):
                    last = dve.scalar_tensor_tensor(dst[:, cb, :], xd[a][:, cb, :], col(which, n, cb), h[a][:, cb, 0:T],
                                                    ALU.mult, ALU.add)
                last.then_inc(ready, 1)

            def mix1(n, used):
                dve.wait_ge(ds_[0], n + 1)
                if used:
                    if later(n):
                        dve.wait_ge(r_done, n)
                mix(xk, 0, TMK, n, mixed1)
                mix(xv, 0, TMV, n, mixed1)
                mix(xr, 0, TMR, n, mixed1)

            def step(i, now, prev, nxt):
                m = i - 1
                if prev:
                    xs = seq(m)
                    dve.wait_ge(wo_done, m + 1)
                    pair = pairs[3][:].rearrange("p a (b c) -> p (a b) c", c=C)
                    dve.scalar_tensor_tensor(xs, pair, 0.5, xs, ALU.mult, ALU.add).then_inc(x_mid, 1)
                    held(dve, spare[:], x_mid, m + 1)
                    norm_stats(1, m)
                if now:
                    dve.wait_ge(k_copied, i + 1)
                    for cb in range(CB):
                        last = dve.tensor_tensor_scan(pp[:, cb, 1:], col(DECAY, i, cb).to_broadcast([P, T]), k_sb[:, cb, :],
                                                      NEG, ALU.add, ALU.max)
                    last.then_inc(pp_ready, 1)
                if prev:
                    normalise(1, m)
                if now:
                    dve.wait_ge(pp_ready, i + 1)
                    dve.tensor_tensor(e2b[:], k_sb[:], pp[:, :, 1:], ALU.subtract).then_inc(e2_arg, 1)
                    for cb in range(CB):
                        last = dve.scalar_tensor_tensor(nd[:, cb, :], k_sb[:, cb, :], col(FIRST, i, cb), pp[:, cb, 0:T],
                                                        ALU.add, ALU.subtract)
                    last.then_inc(nd_ready, 1)
                    dve.wait_ge(nd_ready, i + 1)
                    dve.tensor_scalar(e12[:, 0], nd[:], -1.0, 0.0, ALU.mult, ALU.min).then_inc(e12_arg, 1)
                    dve.tensor_scalar(e12[:, 1], nd[:], 0.0, None, ALU.min).then_inc(e12_arg, 1)
                if prev:
                    dve.wait_ge(ds_[1], m + 1)
                    if now:
                        pass
                    if later(4 * m):
                        dve.wait_ge(ck_done, 4 * m)
                    mix(xr2, 1, CMR, m, mixed2)
                    mix(xk2, 1, CMK, m, mixed2)
                if now:
                    dve.wait_ge(e2b_ready, i + 1)
                    dve.wait_ge(v_copied, i + 1)
                    dve.wait_ge(e12_arg, 2 * i + 2)
                    dve.tensor_tensor(nd[:], e2b[:], v_sb[:], ALU.mult).then_inc(ev_ready, 1)
                    dve.wait_ge(e1b_ready, i + 1)
                    for cb in range(CB):
                        last = dve.tensor_tensor_scan(bb[:, cb, 1:], e1b[:, cb, :], e2b[:, cb, :], 0.0, ALU.mult, ALU.add)
                    last.then_inc(states, 1)
                    dve.wait_ge(ev_ready, i + 1)
                    for cb in range(CB):
                        last = dve.tensor_tensor_scan(aa[:, cb, 1:], e1b[:, cb, :], nd[:, cb, :], 0.0, ALU.mult, ALU.add)
                    last.then_inc(states, 1)
                    dve.wait_ge(e12_ready, i + 1)
                    dve.tensor_tensor(v_sb[:], v_sb[:], e12[:, 1], ALU.mult).then_inc(m2_ready, 1)
                    dve.wait_ge(states, 2 * i + 2)
                    dve.tensor_tensor(m1[:], aa[:, :, 0:T], e12[:, 0], ALU.mult).then_inc(m1_ready, 1)
                    dve.tensor_tensor(e12[:, 0], bb[:, :, 0:T], e12[:, 0], ALU.mult).then_inc(m3_ready, 1)
                    dve.wait_ge(m1_ready, i + 1)
                    dve.wait_ge(m2_ready, i + 1)
                    dve.tensor_tensor(m1[:], m1[:], v_sb[:], ALU.add).then_inc(num_ready, 1)
                    dve.wait_ge(m3_ready, i + 1)
                    dve.tensor_tensor(e12[:, 0], e12[:, 0], e12[:, 1], ALU.add).then_inc(den_ready, 1)
                if nxt:
                    norm_stats(0, i + 1)
                if now:
                    dve.wait_ge(th_ready, i + 1)
                    dve.wait_ge(num_ready, i + 1)
                    dve.scalar_tensor_tensor(m1[:], th[:], 1.0, m1[:], ALU.add, ALU.mult).then_inc(gated, 1)
                if nxt:
                    normalise(0, i + 1)
                if now:
                    dve.wait_ge(rden_ready, i + 1)
                    dve.wait_ge(gated, i + 1)
                    if prev:
                        if later(i):
                            dve.wait_ge(wo_done, i)
                    dve.tensor_tensor(rw[:], m1[:], e12[:, 0], ALU.mult).then_inc(rw_ready, 1)
                if nxt:
                    mix1(i + 1, True)
                if prev:
                    xs = seq(m)
                    dve.wait_ge(cv_done, m + 1)
                    dve.wait_ge(th2_ready, m + 1)
                    t2 = th2[:].rearrange("p (t c) -> p t c", t=TT)
                    pair = pairs[2][:].rearrange("p a (b c) -> p (a b) c", c=C)
                    dve.scalar_tensor_tensor(t2, t2, 1.0, pair, ALU.add, ALU.mult).then_inc(gated2, 1)
                    dve.wait_ge(gated2, m + 1)
                    dve.scalar_tensor_tensor(xs, t2, 0.5, xs, ALU.mult, ALU.add).then_inc(x_done, 1)

            for a in range(2):
                dve.memset(h[a][:, :, 0:1], 0.0).then_inc(edges, 1)
            dve.memset(pp[:, :, 0:1], NEG).then_inc(edges, 1)
            dve.memset(aa[:, :, 0:1], 0.0).then_inc(edges, 1)
            dve.memset(bb[:, :, 0:1], 0.0).then_inc(edges, 1)
            dve.wait_ge(par_exp, 1)
            dve.tensor_scalar(par[:, DECAY], par[:, DECAY], -1.0, None, ALU.mult).then_inc(par_ready, 1)
            norm_stats(0, 0)
            normalise(0, 0)
            mix1(0, False)
            pipeline(dve, step)


def experts(nc, x, ident, eps_pow, x_in, wc_in, bctie_in, w1_in, b1_in, w2_in, b2_in, out):
    ctx = ExitStack()
    with ctx:
        def sb(name, shape):
            return ctx.enter_context(nc.sbuf_tensor(name, shape, F32))

        def sem(name):
            return ctx.enter_context(nc.semaphore(name))

        spare = sb("spare2", [P, 1])
        wc = sb("wc", [P, CB, ES])
        bct = sb("bct", [P, 1 + T])
        w1 = sb("w1", [P, CB, ES, EF])
        w2 = sb("w2", [P, E_, C])
        b1 = sb("b1", [P, E_])
        b2 = sb("b2", [P, C])
        st, mv = sb("st_e", [P, CTT, 6]), sb("mv_e", [P, CTT, 2])
        ve, rstd = sb("ve_e", [P, CTT]), sb("rstd_e", [P, CTT])
        xo = sb("xo", [P, CTT, C])
        xnT = sb("xnT", [P, CB, T])
        lg = sb("lg", [P, CH, T])
        gmax = sb("gmax", [P, CH, T // G])
        pT = sb("pT", [P, 2, ES])
        big = sb("big", [P, CB * ES * NG])
        perm_x = big[:].rearrange("p (cb es n) -> p cb es n", cb=CB, es=ES)
        res_t = big[:].rearrange("p (n cb es) -> p n cb es", cb=CB, es=ES)
        inner = sb("inner", [P, E_, NG])
        res = sb("res", [P, 2, C])
        ps_lg = ctx.enter_context(nc.psum_tensor("ps_lg", [P, 2, 512], F32))
        ps_a = ctx.enter_context(nc.psum_tensor("ps_a", [P, 4, 512], F32))
        ps_o = ctx.enter_context(nc.psum_tensor("ps_o", [P, 2, 512], F32))

        loaded, xo_loaded, x1_done = sem("loaded"), sem("xo_loaded"), sem("x1_done")
        stats, aggr, var, rs, xn = sem("stats_e"), sem("aggr_e"), sem("var_e"), sem("rs_e"), sem("xn_e")
        trd, xT, lgd, lgs, gm, perm = sem("trd"), sem("xT"), sem("lgd"), sem("lgs"), sem("gm"), sem("perm")
        pTd, pTc, gat, gatc = sem("pTd"), sem("pTc"), sem("gat"), sem("gatc")
        w1d, b1d, inn = sem("w1d"), sem("b1d"), sem("inn")
        w2d, resT, rtd, rc, od, fin, stored = (sem("w2d"), sem("resT"), sem("rtd"), sem("rc"), sem("od"), sem("fin"),
                                               sem("stored"))
        block = ctx.enter_context(nc.Block())

        def rows(c):
            return x[:, bass.ds(c * CH, CH), :, :].rearrange("p s t c -> p (s t) c")

        W1G = 16
        W2E = 512 // (CB * NG)

        @block.sync
        def _(sp):
            for dst, src in ((wc, wc_in), (bct, bctie_in), (w1, w1_in), (b1, b1_in), (w2, w2_in), (b2, b2_in)):
                sp.dma_start(dst[:], src).then_inc(loaded, 16)

            def chunk(c):
                if later(CTT * c):
                    sp.wait_ge(gat, CTT * c)
                sp.dma_start(xo[:], x_in[bass.ds(c * CH, CH)].rearrange("s (t p) c -> p (s t) c", p=P)).then_inc(xo_loaded, 16)
                sp.wait_ge(fin, CTT * c + CTT)
                sp.dma_start(out[bass.ds(c * CH, CH)].rearrange("s (t p) c -> p (s t) c", p=P), rows(c)).then_inc(stored, 16)

            chunk(0)
            with sp.Fori(1, CHUNKS) as c:
                chunk(c)

            sp.wait_ge(stored, 16 * CHUNKS)

        @block.gpsimd
        def _(pool):

            def chunk(c):
                pool.wait_ge(var, c + 1)
                pool.tensor_tensor(rstd[:], ve[:], eps_pow[:, 0:CTT], ALU.pow).then_inc(rs, 1)

            chunk(0)
            with pool.Fori(1, CHUNKS) as c:
                chunk(c)

        @block.tensor
        def _(pe):
            pe.wait_ge(loaded, 96)

            def chunk(c):
                pe.wait_ge(xn, c + 1)
                for s in range(CH):
                    n = CH * c + s
                    if later(n):
                        pe.wait_ge(lgs, n)
                    for cb in range(CB):
                        for t in range(TT):
                            last = pe.transpose(ps_lg[:, cb, t * P:(t + 1) * P], xo[:, s * TT + t, cb * P:(cb + 1) * P], ident[:])
                    last.then_inc(trd, 1)
                    pe.wait_ge(xT, n + 1)
                    for cb in range(CB):
                        last = pe.matmul(ps_lg[:, 0, :], wc[:, cb, :], xnT[:, cb, :], start=cb == 0, stop=cb == CB - 1)
                    last.then_inc(lgd, 1)
                pe.wait_ge(perm, c + 1)
                for t in range(CTT):
                    n = CTT * c + t
                    if later(n):
                        pe.wait_ge(pTc, n)
                    pe.transpose(ps_lg[:, 1, 0:P], lg[:, t // TT, (t % TT) * P:(t % TT + 1) * P], ident[:]).then_inc(pTd, 1)
                    pe.wait_ge(pTc, n + 1)
                    if later(n):
                        pe.wait_ge(gatc, n)
                    for g in range(P // G):
                        for cb in range(CB):
                            last = pe.matmul(ps_a[:, g, cb * ES:(cb + 1) * ES], xo[G * g:G * g + G, t, cb * P:(cb + 1) * P],
                                             pT[G * g:G * g + G, 0, :], start=True, stop=True, tile_position=(G * g, 0))
                    last.then_inc(gat, 1)
                pe.wait_ge(gatc, CTT * c + CTT)
                for q in range(E_ // W1G):
                    for e in range(W1G):
                        for s in range(S_):
                            es = (q * W1G + e) * S_ + s
                            for cb in range(CB):
                                last = pe.matmul(ps_a[EF * s:EF * s + EF, q, e * NG:(e + 1) * NG], w1[:, cb, es, :],
                                                 perm_x[:, cb, es, :], start=cb == 0, stop=cb == CB - 1,
                                                 tile_position=(0, EF * s))
                    last.then_inc(w1d, 1)
                for q in range(E_ // W2E):
                    n = E_ // W2E * c + q
                    if q == 0:
                        pe.wait_ge(inn, c + 1)
                    if later(n):
                        pe.wait_ge(resT, n)
                    for j in range(W2E):
                        for s in range(S_):
                            for cb in range(CB):
                                last = pe.matmul(ps_a[:, s, (j * CB + cb) * NG:(j * CB + cb + 1) * NG],
                                                 w2[EF * s:EF * s + EF, q * W2E + j, cb * P:(cb + 1) * P],
                                                 inner[EF * s:EF * s + EF, q * W2E + j, :], start=True, stop=True,
                                                 tile_position=(EF * s, 0))
                    last.then_inc(w2d, 1)
                for g in range(NG):
                    n = NG * c + g
                    if later(n):
                        pe.wait_ge(rc, n)
                    if g == 0:
                        pe.wait_ge(resT, E_ // W2E * (c + 1))
                    for cb in range(CB):
                        last = pe.transpose(ps_lg[:, 1, cb * P:(cb + 1) * P], res_t[:, g, cb, :], ident[:])
                    last.then_inc(rtd, 1)
                    pe.wait_ge(rc, n + 1)
                    t, gg = g // 4, g % 4
                    if gg == 0:
                        if later(CTT * c + t):
                            pe.wait_ge(fin, CTT * c + t)
                    m = pe.matmul(ps_o[G * gg:G * gg + G, 0, 0:C], lg[:, t // TT, ((t % TT) * 4 + gg) * G:((t % TT) * 4 + gg + 1) * G],
                                  res[:, 0, :], start=True, stop=True, tile_position=(0, G * gg))
                    m.then_inc(od, 1)

            chunk(0)
            with pe.Fori(1, CHUNKS) as c:
                chunk(c)

        @block.scalar
        def _(act):

            def chunk(c):
                for s in range(CH):
                    n = CH * c + s
                    act.wait_ge(trd, n + 1)
                    if later(n):
                        act.wait_ge(lgd, n)
                    act.activation(xnT[:], ps_lg[:], ACT.Identity).then_inc(xT, 1)
                for t in range(CTT):
                    n = CTT * c + t
                    act.wait_ge(gat, n + 1)
                    if t == 0:
                        if later(NG * c):
                            act.wait_ge(rtd, NG * c)
                    for cb in range(CB):
                        last = act.activation(perm_x[:, cb, :, 4 * t:4 * t + 4],
                                              ps_a[:, :, cb * ES:(cb + 1) * ES].rearrange("p g es -> p es g"), ACT.Identity)
                    last.then_inc(gatc, 1)

            chunk(0)
            with act.Fori(1, CHUNKS) as c:
                chunk(c)

        @block.vector
        def _(dve):
            dve.wait_ge(loaded, 96)

            def chunk(c):
                xs = rows(c)
                dve.wait_ge(xo_loaded, 16 * c + 16)
                dve.tensor_tensor(xs, xs, xo[:], ALU.add).then_inc(x1_done, 1)
                held(dve, spare[:], x1_done, c + 1)
                for t in range(CTT):
                    last = dve.bn_stats(st[:, t, :], xs[:, t, :])
                last.then_inc(stats, 1)
                held(dve, spare[:], stats, c + 1)
                for t in range(CTT):
                    last = dve.bn_aggr(mv[:, t, :], st[:, t, :])
                last.then_inc(aggr, 1)
                dve.wait_ge(aggr, c + 1)
                dve.tensor_scalar(ve[:], mv[:, :, 1], EPS, None, ALU.add).then_inc(var, 1)
                dve.wait_ge(rs, c + 1)
                for t in range(CTT):
                    last = dve.tensor_scalar(xo[:, t, :], xs[:, t, :], mv[:, t, 0:1], rstd[:, t:t + 1], ALU.subtract, ALU.mult)
                last.then_inc(xn, 1)
                for s in range(CH):
                    n = CH * c + s
                    dve.wait_ge(lgd, n + 1)
                    if s == 0:
                        if later(NG * c):
                            dve.wait_ge(od, NG * c)
                    dve.scalar_tensor_tensor(lg[:, s, :], ps_lg[:, 0, :], bct[:, 0:1], bct[:, 1:], ALU.add, ALU.add)\
                       .then_inc(lgs, 1)
                    dve.wait_ge(lgs, n + 1)
                    l3 = lg[:, s, :].rearrange("p (n t) -> p n t", t=G)
                    dve.tensor_reduce(gmax[:, s, :], l3, AX.X, ALU.max).then_inc(gm, 1)
                    dve.wait_ge(gm, n + 1)
                    last = dve.tensor_tensor(l3, l3, gmax[:, s, :].unsqueeze(2).to_broadcast([P, T // G, G]), ALU.is_equal)
                last.then_inc(perm, 1)
                for t in range(CTT):
                    n = CTT * c + t
                    dve.wait_ge(pTd, n + 1)
                    if later(n):
                        dve.wait_ge(gat, n)
                    dve.tensor_copy(pT[:, 0, :], ps_lg[:, 1, 0:P]).then_inc(pTc, 1)
                for q in range(E_ // W1G):
                    n = E_ // W1G * c + q
                    dve.wait_ge(w1d, n + 1)
                    i3 = inner[:, q * W1G:(q + 1) * W1G, :]
                    dve.tensor_tensor(i3, ps_a[:, q, :].rearrange("p (e n) -> p e n", e=W1G),
                                      b1[:, q * W1G:(q + 1) * W1G].unsqueeze(2).to_broadcast([P, W1G, NG]), ALU.add)\
                       .then_inc(b1d, 1)
                dve.wait_ge(b1d, E_ // W1G * (c + 1))
                dve.tensor_scalar(inner[:], inner[:], 0.0, None, ALU.max).then_inc(inn, 1)
                for q in range(E_ // W2E):
                    n = E_ // W2E * c + q
                    dve.wait_ge(w2d, n + 1)
                    for s in range(S_):
                        last = dve.tensor_copy(
                            res_t[:, :, :, q * W2E * S_ + s:(q + 1) * W2E * S_:S_].rearrange("p n cb e -> p e cb n"),
                            ps_a[:, s, :].rearrange("p (e cb n) -> p e cb n", e=W2E, cb=CB))
                    last.then_inc(resT, 1)
                for g in range(NG):
                    n = NG * c + g
                    dve.wait_ge(rtd, n + 1)
                    if later(n):
                        dve.wait_ge(od, n)
                    dve.tensor_tensor(res[:, 0, :], ps_lg[:, 1, 0:C], b2[:], ALU.add).then_inc(rc, 1)
                    if g % 4 == 3:
                        t = g // 4
                        dve.wait_ge(od, n + 1)
                        dve.tensor_tensor(xs[:, t, :], xs[:, t, :], ps_o[:, 0, 0:C], ALU.add).then_inc(fin, 1)

            chunk(0)
            with dve.Fori(1, CHUNKS) as c:
                chunk(c)


def kernel(**inputs):
    import numpy as np
    import concourse.bacc as bacc
    from concourse.bass_utils import run_bass_kernel_spmd

    a = {n: np.asarray(v) for n, v in inputs.items()}
    f = np.float32

    def cols(v):
        return v.reshape(LAYERS, CB, P).transpose(2, 0, 1)

    def rows(v, nb):
        l, o, i = v.shape
        return v.transpose(0, 2, 1).reshape(l, nb, P, o).transpose(0, 2, 1, 3).reshape(l, P, nb * o)

    L0 = {n[8:]: v for n, v in a.items() if n.startswith("L0_attn_")}
    names = ["ln1_w", "ln1_b", "ln2_w", "ln2_b", "time_decay", "time_first", "tmk", "tmv", "tmr", "cmk", "cmr"]
    arrays = {
        "x_in": L0["x"],
        "ln0": np.stack([L0["ln0_w"], L0["ln0_b"]]),
        "par_in": np.stack([cols(L0[n]) for n in names], axis=1),
        "kvr_in": np.concatenate([rows(L0[n], CB) for n in ("Wk", "Wv", "Wr")], axis=2),
        "wo_in": rows(L0["Wo"], CB),
        "wck_in": rows(L0["Wck"], CB),
        "wcr_in": rows(L0["Wcr"], CB),
        "wcv_in": rows(L0["Wcv"], FB),
        "ident_in": np.eye(P, dtype=f),
        "wc_in": a["L0_ffn_Wc"].reshape(CB, P, ES).transpose(1, 0, 2),
        "bctie_in": np.concatenate([a["L0_ffn_bc"].reshape(ES, 1),
                                    np.broadcast_to(np.tile(np.linspace(0.0, 1e-6, G, dtype=f), T // G), (ES, T))], axis=1),
        "w1_in": a["L0_ffn_W1"].reshape(ES, CB, P, EF).transpose(2, 1, 0, 3),
        "b1_in": a["L0_ffn_b1"].transpose(1, 2, 0).reshape(S_ * EF, E_),
        "w2_in": a["L0_ffn_W2"].transpose(1, 3, 0, 2).reshape(S_ * EF, E_, C),
        "b2_in": a["L0_ffn_b2"].reshape(ES, C),
    }
    nc = bacc.Bacc("TRN2", target_bir_lowering=False, num_devices=1)
    args = {}
    for n, v in arrays.items():
        arrays[n] = v = np.ascontiguousarray(v)
        args[n] = nc.dram_tensor(n, v.shape, mybir.dt.from_np(v.dtype), kind="ExternalInput").ap()
    args["out"] = nc.dram_tensor("out", (SEQS, T, C), F32, kind="ExternalOutput").ap()
    rwkv_moe(nc, **args)
    r = run_bass_kernel_spmd(nc, [arrays], core_ids=[0])
    return r.results[0]["out"]
```

```python
import concourse.bass as bass
from concourse import mybir
from contextlib import ExitStack

F32 = mybir.dt.float32
ALU = mybir.AluOpType
ACT = mybir.ActivationFunctionType
AX = mybir.AxisListType

P = 128
SEQS, T, C, F = 16, 512, 256, 1024
LAYERS = 4
CB, FB, TT = C // P, F // P, T // P
STEPS = LAYERS * SEQS
EPS = 1e-5
NEG = -1e38
(LN1W, LN1B, LN2W, LN2B, DECAY, FIRST, TMK, TMV, TMR, CMK, CMR) = range(11)
NPAR = 11

SLOTS = 5

G = 32
E_, S_, EF = 32, 4, 32
ES = E_ * S_
CHUNKS = 2
CH = SEQS // CHUNKS
NG = CH * T // G
GT = P // G
OCT = 8


def later(count):
    return not isinstance(count, int) or count > 0


def held(dve, spare, sem, count):
    dve.wait_ge(sem, count)
    dve.memset(spare, 0.0)


def rwkv_moe(nc, x_in, ln0, par_in, kvr_in, wo_in, wck_in, wcr_in, wcv_in, ident_in,
             wc_in, bctie_in, w1_in, b1_in, w2_in, b2_in, out):
    outer = ExitStack()
    with outer:
        ident = outer.enter_context(nc.sbuf_tensor("ident", [P, P], F32))
        eps_pow = outer.enter_context(nc.sbuf_tensor("eps_pow", [P, TT], F32))
        x_mem = nc.dram_tensor("x_mem", (SEQS, T, C), F32, kind="Internal").ap()
        layers(nc, ident, eps_pow, x_mem, x_in, ln0, ident_in, par_in, kvr_in, wo_in, wck_in, wcr_in, wcv_in)
        experts(nc, ident, eps_pow, x_mem, x_in, wc_in, bctie_in, w1_in, b1_in, w2_in, b2_in, out)


def layers(nc, ident, eps_pow, x_mem, x_in, ln0, ident_in, par_in, kvr_in, wo_in, wck_in, wcr_in, wcv_in):
    ctx = ExitStack()
    with ctx:
        def sb(name, shape):
            return ctx.enter_context(nc.sbuf_tensor(name, shape, F32))

        def sem(name):
            return ctx.enter_context(nc.semaphore(name))

        U = [P, CB, T]
        x = sb("x", [P, SLOTS, TT, C])
        spare = sb("spare", [P, 1])
        ln0_sb = sb("ln0_sb", [P, 2, C])
        par = sb("par", [P, NPAR, LAYERS, CB])
        kvr_w = sb("kvr_w", [P, 3, CB, C])
        wo_w = sb("wo_w", [P, CB, C])
        wck_w = sb("wck_w", [P, CB, F])
        wcr_w = sb("wcr_w", [P, CB, C])
        wcv_w = sb("wcv_w", [P, FB, C])

        st = [sb(f"st{a}", [P, TT, 6]) for a in range(4)]
        mv = [sb(f"mv{a}", [P, TT, 2]) for a in range(4)]
        ve = [sb(f"ve{a}", [P, TT]) for a in range(4)]
        rstd = [sb(f"rstd{a}", [P, TT]) for a in range(4)]
        xd = [sb(f"xd{a}", U) for a in range(2)]
        h = [sb(f"h{a}", [P, CB, T + 1]) for a in range(2)]
        xk, xv, xr = sb("xk", U), sb("xv", U), sb("xr", U)
        xk2, xr2 = sb("xk2", U), sb("xr2", U)
        kf = sb("kf", [P, FB, T])
        th2 = sb("th2", [P, 2, TT * C])
        k_sb, v_sb, th = sb("k_sb", U), sb("v_sb", U), sb("th", U)
        pp = sb("pp", [P, CB, T + 1])
        aa = sb("aa", [P, CB, T + 1])
        bb = sb("bb", [P, CB, T + 1])
        e1b, e2b = sb("e1b", U), sb("e2b", U)
        nd = sb("nd", U)
        e12 = sb("e12", [P, 2, CB, T])
        m1, rw = sb("m1", U), sb("rw", U)

        pairs = [ctx.enter_context(nc.psum_tensor(f"pair{a}", [P, 2, 512], F32)) for a in range(4)]

        const_loaded, const_set = sem("const_loaded"), sem("const_set")
        par_loaded, par_exp, par_ready = sem("par_loaded"), sem("par_exp"), sem("par_ready")
        edges = sem("edges")
        x_loaded, x_stored = sem("x_loaded"), sem("x_stored")
        kvr_loaded, wo_loaded, ck_loaded, cv_loaded = sem("kvr_loaded"), sem("wo_loaded"), sem("ck_loaded"), sem("cv_loaded")
        stats = [sem(f"stats{a}") for a in range(4)]
        aggr = [sem(f"aggr{a}") for a in range(4)]
        var = [sem(f"var{a}") for a in range(4)]
        rs = [sem(f"rstd{a}_ready") for a in range(4)]
        xn = [sem(f"xn{a}") for a in range(4)]
        scaled, x_first = sem("scaled"), sem("x_first")
        tr = [sem("tr1"), sem("tr2")]
        hs = [sem("h1_ready"), sem("h2_ready")]
        ds_ = [sem("d1_ready"), sem("d2_ready")]
        mixed1, mixed2 = sem("mixed1"), sem("mixed2")
        k_done, v_done, r_done = sem("k_done"), sem("v_done"), sem("r_done")
        k_copied, v_copied, th_ready = sem("k_copied"), sem("v_copied"), sem("th_ready")
        pp_ready, e1_arg, e2_arg = sem("pp_ready"), sem("e1_arg"), sem("e2_arg")
        nd_ready, e12_arg, e12_ready = sem("nd_ready"), sem("e12_arg"), sem("e12_ready")
        e1b_ready, e2b_ready, ev_ready = sem("e1b_ready"), sem("e2b_ready"), sem("ev_ready")
        states = sem("states")
        m1_ready, m2_ready, m3_ready = sem("m1_ready"), sem("m2_ready"), sem("m3_ready")
        num_ready, den_ready, ln_ready, rden_ready = sem("num_ready"), sem("den_ready"), sem("ln_ready"), sem("rden_ready")
        gated, rw_ready = sem("gated"), sem("rw_ready")
        wo_done, x_mid = sem("wo_done"), sem("x_mid")
        cr_done, th2_ready = sem("cr_done"), sem("th2_ready")
        ck_done, relu_done, kf_ready = sem("ck_done"), sem("relu_done"), sem("kf_ready")
        cv_done, gated2, x_done = sem("cv_done"), sem("gated2"), sem("x_done")
        block = ctx.enter_context(nc.Block())

        def inside(n):
            return not isinstance(n, int) or 0 <= n < STEPS

        def pipeline(engine, step):
            for i in range(3):
                step(i, True)
            with engine.Fori(3, SEQS - 2) as i:
                step(i, True)
            with engine.Fori(SEQS - 2, STEPS - 2) as i:
                step(i, False)
            for i in range(STEPS - 2, STEPS + 2):
                step(i, False)

        def slot(n):
            return x[:, bass.ds(n % SLOTS, 1), :, :].rearrange("p s t c -> p (s t) c")

        def col(which, n, cb):
            return par[:, which, bass.ds(n // SEQS, 1), cb]

        @block.sync
        def _(sp):
            def rows(mem, n):
                return mem[bass.ds(n % SEQS, 1)].rearrange("s (t p) c -> p (s t) c", p=P)

            def load(n, mem):
                if later(n):
                    sp.wait_ge(x_loaded, 16 * n)
                sp.dma_start(slot(n), rows(mem, n)).then_inc(x_loaded, 16)

            def step(i, first):
                if inside(i + 2):
                    if inside(i - 3):
                        sp.wait_ge(x_stored, 16 * i - 32)
                    load(i + 2, x_in if first else x_mem)
                if inside(i - 2):
                    sp.wait_ge(x_done, i - 1)
                    if inside(i - 3):
                        sp.wait_ge(x_stored, 16 * i - 32)
                    sp.dma_start(rows(x_mem, i - 2), slot(i - 2)).then_inc(x_stored, 16)

            def weights(mem, l):
                return mem[bass.ds(l, 1)].rearrange("l p n -> (l p) n")

            def time_weights(l):
                if later(l):
                    sp.wait_ge(r_done, SEQS * l)
                sp.dma_start(kvr_w[:].rearrange("p a b c -> p (a b c)"), weights(kvr_in, l)).then_inc(kvr_loaded, 16)
                if later(l):
                    sp.wait_ge(wo_done, SEQS * l)
                sp.dma_start(wo_w[:].rearrange("p b c -> p (b c)"), weights(wo_in, l)).then_inc(wo_loaded, 16)

            def key_weights(l):
                if later(l):
                    sp.wait_ge(ck_done, 4 * SEQS * l)
                sp.dma_start(wcr_w[:].rearrange("p b c -> p (b c)"), weights(wcr_in, l)).then_inc(ck_loaded, 16)
                sp.dma_start(wck_w[:].rearrange("p b c -> p (b c)"), weights(wck_in, l)).then_inc(ck_loaded, 16)

            def value_weights(l):
                if later(l):
                    sp.wait_ge(cv_done, SEQS * l)
                sp.dma_start(wcv_w[:].rearrange("p b c -> p (b c)"), weights(wcv_in, l)).then_inc(cv_loaded, 16)

            sp.dma_start(par[:], par_in).then_inc(par_loaded, 16)
            sp.dma_start(ln0_sb[:], ln0.unsqueeze(0).to_broadcast([P, 2, C])).then_inc(const_loaded, 16)
            sp.dma_start(ident[:], ident_in).then_inc(const_loaded, 16)
            load(0, x_in)
            load(1, x_in)
            time_weights(0)
            key_weights(0)
            value_weights(0)
            for i in range(3):
                step(i, True)
            with sp.Fori(3, SEQS - 2) as i:
                step(i, True)
            step(SEQS - 2, False)
            step(SEQS - 1, False)
            with sp.Fori(1, LAYERS) as l:
                time_weights(l)
                step(SEQS * l, False)
                key_weights(l)
                step(SEQS * l + 1, False)
                value_weights(l)
                with sp.Fori(2, SEQS - 2) as s:
                    step(SEQS * l + s, False)
                step(SEQS * l + SEQS - 2, False)
                step(SEQS * l + SEQS - 1, False)
            step(STEPS, False)
            step(STEPS + 1, False)
            sp.wait_ge(x_stored, 16 * STEPS)

        @block.tensor
        def _(pe):
            def channel_major(pair, w, inp, blocks, done):
                for j, m in enumerate(blocks):
                    for cb in range(CB):
                        last = pe.matmul(pair[:, j, :], w[:, cb, m * P:(m + 1) * P], inp[:, cb, :],
                                         start=cb == 0, stop=cb == CB - 1)
                last.then_inc(done, 1)

            def token_major(pair, inp, w, nb, done):
                for t in range(TT):
                    for b in range(nb):
                        last = pe.matmul(pair[:, t // 2, (t % 2) * C:(t % 2 + 1) * C], inp[:, b, t * P:(t + 1) * P],
                                         w[:, b, :], start=b == 0, stop=b == nb - 1)
                last.then_inc(done, 1)

            def transposes(pair, a, n):
                pe.wait_ge(xn[a], n + 1)
                xt = xd[a][:].rearrange("p a b -> p (a b)").rearrange("p (t c) -> p t c", t=TT)
                for cb in range(CB):
                    for t in range(TT):
                        last = pe.transpose(pair[:, cb, t * P:(t + 1) * P], xt[:, t, cb * P:(cb + 1) * P], ident[:])
                last.then_inc(tr[a], 1)

            def step(i, first):
                now, prev, old, nxt = inside(i), inside(i - 1), inside(i - 2), inside(i + 1)
                if now:
                    pe.wait_ge(kvr_loaded, 16 * (i // SEQS) + 16)
                    if inside(i - 2):
                        pe.wait_ge(relu_done, 4 * (i - 2) + 2)
                    elif prev:
                        pe.wait_ge(th_ready, i)
                    pe.wait_ge(mixed1, 3 * i + 1)
                    channel_major(pairs[0], kvr_w[:, 0], xk, range(CB), k_done)
                    if inside(i - 2):
                        pe.wait_ge(relu_done, 4 * (i - 2) + 3)
                    pe.wait_ge(mixed1, 3 * i + 2)
                    channel_major(pairs[1], kvr_w[:, 1], xv, range(CB), v_done)
                if prev:
                    if inside(i - 2):
                        pe.wait_ge(relu_done, 4 * (i - 2) + 4)
                    transposes(pairs[2], 1, i - 1)
                if old:
                    pe.wait_ge(cv_loaded, 16 * ((i - 2) // SEQS) + 16)
                    pe.wait_ge(kf_ready, 4 * (i - 2) + 4)
                    if inside(i - 1):
                        pe.wait_ge(x_mid, i)
                    token_major(pairs[3], kf, wcv_w, FB, cv_done)
                if now:
                    pe.wait_ge(k_copied, i + 1)
                    pe.wait_ge(mixed1, 3 * i + 3)
                    channel_major(pairs[0], kvr_w[:, 2], xr, range(CB), r_done)
                if nxt:
                    if now:
                        pe.wait_ge(v_copied, i + 1)
                    transposes(pairs[1], 0, i + 1)
                if prev:
                    pe.wait_ge(ck_loaded, 32 * ((i - 1) // SEQS) + 32)
                    pe.wait_ge(mixed2, 2 * (i - 1) + 1)
                    pe.wait_ge(hs[1], i)
                    token_major(pairs[2], xr2, wcr_w, CB, cr_done)
                    pe.wait_ge(mixed2, 2 * (i - 1) + 2)
                    if old:
                        pe.wait_ge(gated2, i - 1)
                    channel_major(pairs[3], wck_w, xk2, (0, 1), ck_done)
                    if now:
                        pe.wait_ge(th_ready, i + 1)
                    channel_major(pairs[0], wck_w, xk2, (2, 3), ck_done)
                    if nxt:
                        pe.wait_ge(hs[0], i + 2)
                    channel_major(pairs[1], wck_w, xk2, (4, 5), ck_done)
                    pe.wait_ge(th2_ready, i)
                    channel_major(pairs[2], wck_w, xk2, (6, 7), ck_done)
                if now:
                    pe.wait_ge(wo_loaded, 16 * (i // SEQS) + 16)
                    if prev:
                        pe.wait_ge(relu_done, 4 * (i - 1) + 1)
                    pe.wait_ge(rw_ready, i + 1)
                    token_major(pairs[3], rw, wo_w, CB, wo_done)

            pe.wait_ge(const_loaded, 32)
            transposes(pairs[1], 0, 0)
            pipeline(pe, step)

        @block.scalar
        def _(act):
            def affine(pair, a, n, ready):
                act.wait_ge(tr[a], n + 1)
                if later(n):
                    if a:
                        act.wait_ge(mixed2, 2 * n)
                    else:
                        act.wait_ge(mixed1, 3 * n)
                wi, bi = (LN2W, LN2B) if a else (LN1W, LN1B)
                for cb in range(CB):
                    last = act.activation(h[a][:, cb, 1:], pair[:, cb, :], ACT.Identity,
                                          bias=col(bi, n, cb), scale=col(wi, n, cb))
                last.then_inc(ready, 1)

            def relu(m, j):
                act.wait_ge(ck_done, 4 * m + j + 1)
                if not j and later(m):
                    act.wait_ge(cv_done, m)
                act.activation(kf[:, 2 * j:2 * j + 2, :], pairs[(j + 3) % 4][:], ACT.Relu).then_inc(relu_done, 1)

            def step(i, first):
                now, prev, nxt = inside(i), inside(i - 1), inside(i + 1)
                if now:
                    act.wait_ge(k_done, i + 1)
                    if prev:
                        act.wait_ge(rw_ready, i)
                    act.activation(k_sb[:], pairs[0][:], ACT.Identity).then_inc(k_copied, 1)
                    act.wait_ge(v_done, i + 1)
                    act.activation(v_sb[:], pairs[1][:], ACT.Identity).then_inc(v_copied, 1)
                if prev:
                    affine(pairs[2], 1, i - 1, hs[1])
                if now:
                    act.wait_ge(e2_arg, i + 1)
                    act.activation(e2b[:], e2b[:], ACT.Exp).then_inc(e2b_ready, 1)
                    act.wait_ge(e1_arg, i + 1)
                    for cb in range(CB):
                        last = act.activation(e1b[:, cb, :], e1b[:, cb, :], ACT.Exp, bias=col(DECAY, i, cb))
                    last.then_inc(e1b_ready, 1)
                    act.wait_ge(e12_arg, 2 * i + 2)
                    act.activation(e12[:], e12[:], ACT.Exp).then_inc(e12_ready, 1)
                    act.wait_ge(r_done, i + 1)
                    act.activation(th[:], pairs[0][:], ACT.Tanh, scale=0.5).then_inc(th_ready, 1)
                if nxt:
                    affine(pairs[1], 0, i + 1, hs[0])
                if prev:
                    act.wait_ge(cr_done, i)
                    if later(i - 2):
                        act.wait_ge(x_done, i - 2)
                    act.activation(th2[:, bass.ds((i - 1) % 2, 1), :].rearrange("p a b -> p (a b)"),
                                   pairs[2][:].rearrange("p a b -> p (a b)"), ACT.Tanh, scale=0.5).then_inc(th2_ready, 1)
                if now:
                    act.wait_ge(den_ready, i + 1)
                    den = e12[:, 0]
                    act.activation(den, den, ACT.Ln).then_inc(ln_ready, 1)
                    act.wait_ge(ln_ready, i + 1)
                    act.activation(den, den, ACT.Exp, scale=-1.0).then_inc(rden_ready, 1)
                if prev:
                    for j in range(4):
                        relu(i - 1, j)

            act.wait_ge(par_loaded, 16)
            act.activation(par[:, DECAY], par[:, DECAY], ACT.Exp).then_inc(par_exp, 1)
            act.wait_ge(par_ready, 1)
            act.wait_ge(edges, 5)
            affine(pairs[1], 0, 0, hs[0])
            pipeline(act, step)

        @block.gpsimd
        def _(pool):
            def power(a, n):
                pool.wait_ge(var[a], n + 1)
                pool.tensor_tensor(rstd[a][:], ve[a][:], eps_pow[:], ALU.pow).then_inc(rs[a], 1)

            def diff(a, n):
                pool.wait_ge(hs[a], n + 1)
                pool.tensor_tensor(xd[a][:], h[a][:, :, 1:], h[a][:, :, 0:T], ALU.subtract).then_inc(ds_[a], 1)

            def step(i, first):
                if inside(i - 1):
                    power(1, i - 1)
                if inside(i):
                    pool.wait_ge(pp_ready, i + 1)
                    pool.tensor_tensor(e1b[:], pp[:, :, 0:T], pp[:, :, 1:], ALU.subtract).then_inc(e1_arg, 1)
                if inside(i - 1):
                    diff(1, i - 1)
                if inside(i + 1):
                    power(0, i + 1)
                if first:
                    power(2, i + 2)
                if inside(i + 1):
                    diff(0, i + 1)
                if first:
                    power(3, i + 2)
                if inside(i - 1):
                    for j in range(4):
                        pool.wait_ge(relu_done, 4 * (i - 1) + j + 1)
                        pool.tensor_tensor(kf[:, 2 * j:2 * j + 2, :], kf[:, 2 * j:2 * j + 2, :],
                                           kf[:, 2 * j:2 * j + 2, :], ALU.mult).then_inc(kf_ready, 1)

            pool.memset(eps_pow[:], -0.5).then_inc(const_set, 1)
            pool.wait_ge(const_set, 1)
            for n in range(2):
                power(2, n)
                power(3, n)
            power(0, 0)
            diff(0, 0)
            pipeline(pool, step)

        @block.vector
        def _(dve):
            def norm_stats(a, n):
                for t in range(TT):
                    last = dve.bn_stats(st[a][:, t, :], slot(n)[:, t, :])
                last.then_inc(stats[a], 1)
                held(dve, spare[:], stats[a], n + 1)
                for t in range(TT):
                    last = dve.bn_aggr(mv[a][:, t, :], st[a][:, t, :])
                last.then_inc(aggr[a], 1)
                dve.wait_ge(aggr[a], n + 1)
                dve.tensor_scalar(ve[a][:], mv[a][:, :, 1], EPS, None, ALU.add).then_inc(var[a], 1)

            def normalise(a, n, dst):
                dve.wait_ge(rs[a], n + 1)
                for t in range(TT):
                    last = dve.tensor_scalar(dst[:, t, :], slot(n)[:, t, :], mv[a][:, t, 0:1], rstd[a][:, t:t + 1],
                                             ALU.subtract, ALU.mult)
                last.then_inc(xn[a], 1)

            def rows(a):
                return xd[a][:].rearrange("p a b -> p (a b)").rearrange("p (t c) -> p t c", t=TT)

            def first_stats(n):
                held(dve, spare[:], x_loaded, 16 * n + 16)
                norm_stats(2, n)

            def first_norm(n):
                normalise(2, n, slot(n))
                held(dve, spare[:], xn[2], n + 1)
                norm_stats(3, n)

            def second_norm(n):
                normalise(3, n, slot(n))
                dve.wait_ge(xn[3], n + 1)
                dve.tensor_tensor(slot(n), slot(n), ln0_sb[:, 0:1, :].to_broadcast([P, TT, C]), ALU.mult).then_inc(scaled, 1)
                dve.wait_ge(scaled, n + 1)
                dve.tensor_tensor(slot(n), slot(n), ln0_sb[:, 1:2, :].to_broadcast([P, TT, C]), ALU.add).then_inc(x_first, 1)

            def mix(dst, a, which, n, ready):
                for cb in range(CB):
                    last = dve.scalar_tensor_tensor(dst[:, cb, :], xd[a][:, cb, :], col(which, n, cb), h[a][:, cb, 0:T],
                                                    ALU.mult, ALU.add)
                last.then_inc(ready, 1)

            def mix1(n):
                dve.wait_ge(ds_[0], n + 1)
                if later(n):
                    dve.wait_ge(r_done, n)
                mix(xk, 0, TMK, n, mixed1)
                mix(xv, 0, TMV, n, mixed1)
                mix(xr, 0, TMR, n, mixed1)

            def step(i, first):
                now, prev, old, nxt = inside(i), inside(i - 1), inside(i - 2), inside(i + 1)
                if prev:
                    xs = slot(i - 1)
                    dve.wait_ge(wo_done, i)
                    pair = pairs[3][:].rearrange("p a (b c) -> p (a b) c", c=C)
                    dve.scalar_tensor_tensor(xs, pair, 0.5, xs, ALU.mult, ALU.add).then_inc(x_mid, 1)
                    held(dve, spare[:], x_mid, i)
                    norm_stats(1, i - 1)
                if now:
                    dve.wait_ge(k_copied, i + 1)
                    for cb in range(CB):
                        last = dve.tensor_tensor_scan(pp[:, cb, 1:], col(DECAY, i, cb).to_broadcast([P, T]), k_sb[:, cb, :],
                                                      NEG, ALU.add, ALU.max)
                    last.then_inc(pp_ready, 1)
                if prev:
                    normalise(1, i - 1, rows(1))
                if now:
                    dve.wait_ge(pp_ready, i + 1)
                    dve.tensor_tensor(e2b[:], k_sb[:], pp[:, :, 1:], ALU.subtract).then_inc(e2_arg, 1)
                    for cb in range(CB):
                        last = dve.scalar_tensor_tensor(nd[:, cb, :], k_sb[:, cb, :], col(FIRST, i, cb), pp[:, cb, 0:T],
                                                        ALU.add, ALU.subtract)
                    last.then_inc(nd_ready, 1)
                if nxt:
                    if not first:
                        held(dve, spare[:], x_loaded, 16 * (i + 1) + 16)
                    else:
                        held(dve, spare[:], x_first, i + 2)
                    norm_stats(0, i + 1)
                if now:
                    dve.wait_ge(nd_ready, i + 1)
                    dve.tensor_scalar(e12[:, 0], nd[:], -1.0, 0.0, ALU.mult, ALU.min).then_inc(e12_arg, 1)
                    dve.tensor_scalar(e12[:, 1], nd[:], 0.0, None, ALU.min).then_inc(e12_arg, 1)
                if nxt:
                    normalise(0, i + 1, rows(0))
                if now:
                    dve.wait_ge(e2b_ready, i + 1)
                    dve.wait_ge(v_copied, i + 1)
                    dve.wait_ge(e12_arg, 2 * i + 2)
                    dve.tensor_tensor(nd[:], e2b[:], v_sb[:], ALU.mult).then_inc(ev_ready, 1)
                if prev:
                    dve.wait_ge(ds_[1], i)
                    if later(i - 1):
                        dve.wait_ge(ck_done, 4 * (i - 1))
                    mix(xr2, 1, CMR, i - 1, mixed2)
                    mix(xk2, 1, CMK, i - 1, mixed2)
                if now:
                    dve.wait_ge(e1b_ready, i + 1)
                    for cb in range(CB):
                        last = dve.tensor_tensor_scan(bb[:, cb, 1:], e1b[:, cb, :], e2b[:, cb, :], 0.0, ALU.mult, ALU.add)
                    last.then_inc(states, 1)
                    dve.wait_ge(ev_ready, i + 1)
                    for cb in range(CB):
                        last = dve.tensor_tensor_scan(aa[:, cb, 1:], e1b[:, cb, :], nd[:, cb, :], 0.0, ALU.mult, ALU.add)
                    last.then_inc(states, 1)
                    dve.wait_ge(e12_ready, i + 1)
                    dve.tensor_tensor(v_sb[:], v_sb[:], e12[:, 1], ALU.mult).then_inc(m2_ready, 1)
                    dve.wait_ge(states, 2 * i + 2)
                    dve.tensor_tensor(m1[:], aa[:, :, 0:T], e12[:, 0], ALU.mult).then_inc(m1_ready, 1)
                    dve.tensor_tensor(e12[:, 0], bb[:, :, 0:T], e12[:, 0], ALU.mult).then_inc(m3_ready, 1)
                    dve.wait_ge(m1_ready, i + 1)
                    dve.wait_ge(m2_ready, i + 1)
                    dve.tensor_tensor(m1[:], m1[:], v_sb[:], ALU.add).then_inc(num_ready, 1)
                    dve.wait_ge(m3_ready, i + 1)
                    dve.tensor_tensor(e12[:, 0], e12[:, 0], e12[:, 1], ALU.add).then_inc(den_ready, 1)
                if first:
                    first_stats(i + 2)
                if old:
                    xs = slot(i - 2)
                    dve.wait_ge(cv_done, i - 1)
                    dve.wait_ge(th2_ready, i - 1)
                    t2 = th2[:, bass.ds(i % 2, 1), :].rearrange("p a (t c) -> p (a t) c", t=TT)
                    pair = pairs[3][:].rearrange("p a (b c) -> p (a b) c", c=C)
                    dve.scalar_tensor_tensor(t2, t2, 1.0, pair, ALU.add, ALU.mult).then_inc(gated2, 1)
                    dve.wait_ge(gated2, i - 1)
                    dve.scalar_tensor_tensor(xs, t2, 0.5, xs, ALU.mult, ALU.add).then_inc(x_done, 1)
                if now:
                    dve.wait_ge(th_ready, i + 1)
                    dve.wait_ge(num_ready, i + 1)
                    dve.scalar_tensor_tensor(m1[:], th[:], 1.0, m1[:], ALU.add, ALU.mult).then_inc(gated, 1)
                if first:
                    first_norm(i + 2)
                if nxt:
                    mix1(i + 1)
                if now:
                    dve.wait_ge(rden_ready, i + 1)
                    dve.wait_ge(gated, i + 1)
                    if prev:
                        dve.wait_ge(wo_done, i)
                    dve.tensor_tensor(rw[:], m1[:], e12[:, 0], ALU.mult).then_inc(rw_ready, 1)
                if first:
                    second_norm(i + 2)

            for a in range(2):
                dve.memset(h[a][:, :, 0:1], 0.0).then_inc(edges, 1)
            dve.memset(pp[:, :, 0:1], NEG).then_inc(edges, 1)
            dve.memset(aa[:, :, 0:1], 0.0).then_inc(edges, 1)
            dve.memset(bb[:, :, 0:1], 0.0).then_inc(edges, 1)
            dve.wait_ge(par_exp, 1)
            dve.tensor_scalar(par[:, DECAY], par[:, DECAY], -1.0, None, ALU.mult).then_inc(par_ready, 1)
            dve.wait_ge(const_loaded, 32)
            for n in range(2):
                first_stats(n)
                first_norm(n)
                second_norm(n)
            held(dve, spare[:], x_first, 1)
            norm_stats(0, 0)
            normalise(0, 0, rows(0))
            mix1(0)
            pipeline(dve, step)


def experts(nc, ident, eps_pow, x_mem, x_in, wc_in, bctie_in, w1_in, b1_in, w2_in, b2_in, out):
    ctx = ExitStack()
    with ctx:
        def sb(name, shape):
            return ctx.enter_context(nc.sbuf_tensor(name, shape, F32))

        def sem(name):
            return ctx.enter_context(nc.semaphore(name))

        spare = sb("spare_e", [P, 1])
        wc = sb("wc", [P, CB, ES])
        bct = sb("bct", [P, 1 + G])
        b1 = sb("b1", [P, E_])
        b2 = sb("b2", [P, C])
        st, mv = sb("st_e", [P, TT, 6]), sb("mv_e", [P, TT, 2])
        ve, rstd = sb("ve_e", [P, TT]), sb("rstd_e", [P, TT])
        xa = sb("xa", [P, 2, TT, C])
        xi = sb("xi", [P, 2, TT, C])
        gmax = sb("gmax", [P, T // G])
        perm = sb("perm", [P, CH, T])
        work = sb("work", [P, 2 * TT * C])
        xnT = work[:, 0:CB * T].rearrange("p (cb t) -> p cb t", cb=CB)
        pT = work[:, CB * T:CB * T + 2 * TT * ES].rearrange("p (b t es) -> p b t es", b=2, t=TT)
        res = work[:].rearrange("p (b g c) -> p b g c", b=2, g=GT)
        big = sb("big", [P, CB * ES * NG])
        perm_x = big[:].rearrange("p (cb es n) -> p cb es n", cb=CB, es=ES)
        res_t = big[:].rearrange("p (n cb es) -> p n cb es", cb=CB, es=ES)
        inner = sb("inner", [P, E_, NG])
        ring = sb("ring", [P, 2, OCT * C])
        w1 = ring[:].rearrange("p b (cb es f) -> p b cb es f", cb=CB, es=OCT * S_)
        w2 = ring[:].rearrange("p b (e c) -> p b e c", e=OCT)
        banks = [ctx.enter_context(nc.psum_tensor(f"bank{a}", [P, 512], F32)) for a in range(8)]

        x1_mem = nc.dram_tensor("x1_mem", (SEQS, T, C), F32, kind="Internal").ap()
        NOCT = E_ // OCT
        loaded, chunk_free = sem("loaded"), sem("chunk_free")
        xo_loaded, x1_done, x1_stored = sem("xo_loaded"), sem("x1_done"), sem("x1_stored")
        stats, aggr, var, rs, xn = sem("stats_e"), sem("aggr_e"), sem("var_e"), sem("rs_e"), sem("xn_e")
        trd, xT, lgd, lgs, gm, perm_ok = sem("trd"), sem("xT"), sem("lgd"), sem("lgs"), sem("gm"), sem("perm_ok")
        pTd, pTc = sem("pTd"), sem("pTc")
        gat = sem("gat")
        gat_act, gat_dve = sem("gat_act"), sem("gat_dve")
        w_loaded, w1d, inn = sem("w_loaded"), sem("w1d"), sem("inn")
        w2d, res_act, res_dve = sem("w2d"), sem("res_act"), sem("res_dve")
        rtd, rc, od, fin = sem("rtd"), sem("rc"), sem("od"), sem("fin")
        xr_loaded, stored = sem("xr_loaded"), sem("stored")
        block = ctx.enter_context(nc.Block())

        def dram_rows(mem, n):
            return mem[bass.ds(n, 1)].rearrange("s (t p) c -> p (s t) c", p=P)

        B1 = E_ // 4
        C1 = E_ // 2
        TD = CH * TT

        @block.sync
        def _(sp):
            for dst, src in ((wc, wc_in), (bct, bctie_in), (b1, b1_in), (b2, b2_in)):
                sp.dma_start(dst[:], src).then_inc(loaded, 16)

            def fetch(c, s):
                n = CH * c + s
                if n:
                    sp.wait_ge(xo_loaded, 32 * n)
                sp.dma_start(xa[:, s % 2], dram_rows(x_mem, n)).then_inc(xo_loaded, 16)
                sp.dma_start(xi[:, s % 2], dram_rows(x_in, n)).then_inc(xo_loaded, 16)

            def weights(mem, c, k, q):
                if c or k:
                    sp.wait_ge(w_loaded, 16 * (2 * NOCT * c + k))
                sp.dma_start(ring[:, k % 2], mem[q]).then_inc(w_loaded, 16)

            for c in range(CHUNKS):
                sp.wait_ge(chunk_free, c + 1)
                weights(w1_in, c, 0, 0)
                weights(w1_in, c, 1, 1)
                fetch(c, 0)
                for s in range(1, CH):
                    if s >= 2:
                        sp.wait_ge(gat, 2 * (CH * c + s) - 2)
                        sp.wait_ge(x1_stored, 16 * (CH * c + s - 1))
                    fetch(c, s)
                    sp.wait_ge(x1_done, CH * c + s)
                    if CH * c + s - 1 > 0:
                        sp.wait_ge(x1_stored, 16 * (CH * c + s - 1))
                    sp.dma_start(dram_rows(x1_mem, CH * c + s - 1), xa[:, (s - 1) % 2]).then_inc(x1_stored, 16)
                sp.wait_ge(x1_done, CH * c + CH)
                sp.wait_ge(x1_stored, 16 * (CH * c + CH - 1))
                sp.dma_start(dram_rows(x1_mem, CH * c + CH - 1), xa[:, (CH - 1) % 2]).then_inc(x1_stored, 16)
                sp.wait_ge(xn, CH * c + CH)
                for k in range(2, 2 * NOCT):
                    if k < NOCT + 2:
                        sp.wait_ge(w1d, B1 * c + (k - 1) * (OCT // 4))
                    else:
                        sp.wait_ge(w2d, C1 * c + (k - 1 - NOCT) * (OCT // 2))
                    weights(w1_in if k < NOCT else w2_in, c, k, k % NOCT)
                for s in range(CH):
                    n = CH * c + s
                    if s >= 2:
                        sp.wait_ge(stored, 16 * (n - 1))
                    if n:
                        sp.wait_ge(xr_loaded, 16 * n)
                    if s == 0:
                        sp.wait_ge(x1_stored, 16 * (CH * c + CH))
                    sp.dma_start(xa[:, s % 2], dram_rows(x1_mem, n)).then_inc(xr_loaded, 16)
                    if s:
                        sp.wait_ge(fin, TT * n)
                        sp.dma_start(dram_rows(out, n - 1), xa[:, (s - 1) % 2]).then_inc(stored, 16)
                sp.wait_ge(fin, TT * (CH * c + CH))
                sp.wait_ge(stored, 16 * (CH * c + CH - 1))
                sp.dma_start(dram_rows(out, CH * c + CH - 1), xa[:, (CH - 1) % 2]).then_inc(stored, 16)
            sp.wait_ge(stored, 16 * SEQS)

        @block.gpsimd
        def _(pool):
            with pool.Fori(0, SEQS) as n:
                pool.wait_ge(var, n + 1)
                pool.tensor_tensor(rstd[:], ve[:], eps_pow[:], ALU.pow).then_inc(rs, 1)

        @block.tensor
        def _(pe):
            pe.wait_ge(loaded, 64)

            def transpose_norm(c, s):
                n = CH * c + s
                pe.wait_ge(xn, n + 1)
                if s:
                    pe.wait_ge(xT, n)
                for cb in range(CB):
                    for t in range(TT):
                        last = pe.transpose(banks[cb][:, t * P:(t + 1) * P], xi[:, s % 2, t, cb * P:(cb + 1) * P], ident[:])
                last.then_inc(trd, 1)

            def logits(c, s):
                n = CH * c + s
                pe.wait_ge(xT, n + 1)
                if s:
                    pe.wait_ge(lgs, n)
                for cb in range(CB):
                    last = pe.matmul(banks[2][:], wc[:, cb, :], xnT[:, cb, :], start=cb == 0, stop=cb == CB - 1)
                last.then_inc(lgd, 1)

            def transpose_perm(c, s):
                n = CH * c + s
                pe.wait_ge(perm_ok, n + 1)
                if s:
                    pe.wait_ge(pTc, n)
                for t in range(TT):
                    last = pe.transpose(banks[3][:, t * P:(t + 1) * P], perm[:, s, t * P:(t + 1) * P], ident[:])
                last.then_inc(pTd, 1)

            def gather(c, s, r):
                k = 2 * s + r
                if r == 0:
                    pe.wait_ge(pTc, CH * c + s + 1)
                if k:
                    pe.wait_ge(gat_act, 2 * CH * c + k)
                    pe.wait_ge(gat_dve, 2 * CH * c + k)
                for t in range(2):
                    for g in range(GT):
                        for cb in range(CB):
                            last = pe.matmul(banks[4 + g][:, (t * CB + cb) * ES:(t * CB + cb + 1) * ES],
                                             xi[G * g:G * g + G, s % 2, 2 * r + t, cb * P:(cb + 1) * P],
                                             pT[G * g:G * g + G, s % 2, 2 * r + t, :], start=True, stop=True,
                                             tile_position=(G * g, 0))
                last.then_inc(gat, 1)

            with pe.Fori(0, CHUNKS) as c:
                pe.wait_ge(chunk_free, c + 1)
                transpose_norm(c, 0)
                logits(c, 0)
                transpose_perm(c, 0)
                for s in range(CH):
                    if s + 1 < CH:
                        transpose_norm(c, s + 1)
                    gather(c, s, 0)
                    if s + 1 < CH:
                        logits(c, s + 1)
                    gather(c, s, 1)
                    if s + 1 < CH:
                        transpose_perm(c, s + 1)
                pe.wait_ge(gat_act, 2 * CH * (c + 1))
                pe.wait_ge(gat_dve, 2 * CH * (c + 1))
                for q in range(B1):
                    if q % (OCT // 4) == 0:
                        pe.wait_ge(w_loaded, 16 * (2 * NOCT * c + q // (OCT // 4)) + 16)
                    if q >= 4:
                        pe.wait_ge(inn, E_ * c + 4 * (q - 3))
                    for j in range(4):
                        e = 4 * q + j
                        for cb in range(CB):
                            for s in range(S_):
                                last = pe.matmul(banks[4 + q % 4][EF * s:EF * s + EF, j * NG:(j + 1) * NG],
                                                 w1[:, (e // OCT) % 2, cb, (e % OCT) * S_ + s, :],
                                                 perm_x[:, cb, e * S_ + s, :], start=cb == 0, stop=cb == CB - 1,
                                                 tile_position=(0, EF * s))
                    last.then_inc(w1d, 1)
                for q in range(C1):
                    if q % (OCT // 2) == 0:
                        pe.wait_ge(w_loaded, 16 * (2 * NOCT * c + NOCT + q // (OCT // 2)) + 16)
                    if q == 0:
                        pe.wait_ge(inn, E_ * (c + 1))
                    if q >= 2:
                        pe.wait_ge(res_act, C1 * c + q - 1)
                        pe.wait_ge(res_dve, C1 * c + q - 1)
                    for j in range(2):
                        e = 2 * q + j
                        for s in range(S_):
                            for cb in range(CB):
                                last = pe.matmul(banks[4 * (q % 2) + s][:, (j * CB + cb) * NG:(j * CB + cb + 1) * NG],
                                                 w2[EF * s:EF * s + EF, (e // OCT) % 2, e % OCT, cb * P:(cb + 1) * P],
                                                 inner[EF * s:EF * s + EF, e, :], start=True, stop=True,
                                                 tile_position=(EF * s, 0))
                    last.then_inc(w2d, 1)
                pe.wait_ge(res_act, C1 * (c + 1))
                pe.wait_ge(res_dve, C1 * (c + 1))

                def back(t):
                    if t >= 2:
                        pe.wait_ge(rc, 2 * (TD * c + t - 1))
                    for g in range(GT):
                        for cb in range(CB):
                            last = pe.transpose(banks[2 * (t % 2) + g // 2][:, ((g % 2) * CB + cb) * P:((g % 2) * CB + cb + 1) * P],
                                                res_t[:, GT * t + g, cb, :], ident[:])
                    last.then_inc(rtd, 1)

                back(0)
                for t in range(TD):
                    if t + 1 < TD:
                        back(t + 1)
                    pe.wait_ge(rc, 2 * (TD * c + t) + 2)
                    if t >= 2:
                        pe.wait_ge(fin, TD * c + t - 1)
                    for g in range(GT):
                        last = pe.matmul(banks[4 + t % 2][G * g:G * g + G, 0:C],
                                         perm[:, t // TT, (t % TT) * P + g * G:(t % TT) * P + (g + 1) * G],
                                         res[:, t % 2, g, :], start=True, stop=True, tile_position=(0, G * g))
                    last.then_inc(od, 1)

        @block.scalar
        def _(act):
            with act.Fori(0, CHUNKS) as c:
                act.wait_ge(chunk_free, c + 1)

                def channels(s):
                    n = CH * c + s
                    act.wait_ge(trd, n + 1)
                    if s:
                        act.wait_ge(lgd, n)
                    for cb in range(CB):
                        last = act.activation(xnT[:, cb, :], banks[cb][:], ACT.Identity)
                    last.then_inc(xT, 1)

                def perm_rows(s):
                    act.wait_ge(pTd, CH * c + s + 1)
                    if s >= 2:
                        act.wait_ge(gat, 2 * (CH * c + s) - 2)
                    act.activation(pT[:, s % 2], banks[3][:].rearrange("p (t es) -> p t es", t=TT), ACT.Identity).then_inc(pTc, 1)

                channels(0)
                perm_rows(0)
                for s in range(CH):
                    if s + 1 < CH:
                        channels(s + 1)
                    for r in range(2):
                        act.wait_ge(gat, 2 * (CH * c + s) + r + 1)
                        for g in range(2):
                            n0 = GT * (TT * s + 2 * r) + g
                            last = act.activation(perm_x[:, :, :, n0:n0 + GT + 1:GT].rearrange("p cb es t -> p t cb es"),
                                                  banks[4 + g][:].rearrange("p (t cb es) -> p t cb es", t=2, cb=CB), ACT.Identity)
                        last.then_inc(gat_act, 1)
                    if s + 1 < CH:
                        perm_rows(s + 1)
                for q in range(C1):
                    act.wait_ge(w2d, C1 * c + q + 1)
                    for s in range(2):
                        last = act.activation(
                            res_t[:, :, :, 2 * q * S_ + s:2 * q * S_ + s + S_ + 1:S_].rearrange("p n cb e -> p e cb n"),
                            banks[4 * (q % 2) + s][:].rearrange("p (e cb n) -> p e cb n", e=2, cb=CB), ACT.Identity)
                    last.then_inc(res_act, 1)

        @block.vector
        def _(dve):
            dve.wait_ge(loaded, 64)
            dve.memset(spare[:], 0.0).then_inc(chunk_free, 1)
            with dve.Fori(0, CHUNKS) as c:
                def norm(s):
                    n = CH * c + s
                    dve.wait_ge(xo_loaded, 32 * n + 32)
                    xs, xw = xa[:, s % 2], xi[:, s % 2]
                    dve.tensor_tensor(xs, xs, xw, ALU.add).then_inc(x1_done, 1)
                    held(dve, spare[:], x1_done, n + 1)
                    for t in range(TT):
                        last = dve.bn_stats(st[:, t, :], xs[:, t, :])
                    last.then_inc(stats, 1)
                    held(dve, spare[:], stats, n + 1)
                    for t in range(TT):
                        last = dve.bn_aggr(mv[:, t, :], st[:, t, :])
                    last.then_inc(aggr, 1)
                    dve.wait_ge(aggr, n + 1)
                    dve.tensor_scalar(ve[:], mv[:, :, 1], EPS, None, ALU.add).then_inc(var, 1)
                    dve.wait_ge(rs, n + 1)
                    for t in range(TT):
                        last = dve.tensor_scalar(xw[:, t, :], xs[:, t, :], mv[:, t, 0:1], rstd[:, t:t + 1],
                                                 ALU.subtract, ALU.mult)
                    last.then_inc(xn, 1)

                def choose(s):
                    n = CH * c + s
                    dve.wait_ge(lgd, n + 1)
                    l3 = perm[:, s, :].rearrange("p (n t) -> p n t", t=G)
                    dve.scalar_tensor_tensor(l3, banks[2][:].rearrange("p (n t) -> p n t", t=G), bct[:, 0:1],
                                             bct[:, 1:].unsqueeze(1).to_broadcast([P, T // G, G]), ALU.add, ALU.add)\
                       .then_inc(lgs, 1)
                    dve.wait_ge(lgs, n + 1)
                    dve.tensor_reduce(gmax[:], l3, AX.X, ALU.max).then_inc(gm, 1)
                    dve.wait_ge(gm, n + 1)
                    dve.tensor_tensor(l3, l3, gmax[:].unsqueeze(2).to_broadcast([P, T // G, G]), ALU.is_equal).then_inc(perm_ok, 1)

                norm(0)
                choose(0)
                norm(1)
                for s in range(CH):
                    for r in range(2):
                        dve.wait_ge(gat, 2 * (CH * c + s) + r + 1)
                        for g in range(2, GT):
                            n0 = GT * (TT * s + 2 * r) + g
                            last = dve.tensor_copy(perm_x[:, :, :, n0:n0 + GT + 1:GT].rearrange("p cb es t -> p t cb es"),
                                                   banks[4 + g][:].rearrange("p (t cb es) -> p t cb es", t=2, cb=CB))
                        last.then_inc(gat_dve, 1)
                        if r == 0 and s + 1 < CH:
                            choose(s + 1)
                    if s + 2 < CH:
                        norm(s + 2)
                for e in range(E_):
                    if e % 4 == 0:
                        dve.wait_ge(w1d, B1 * c + e // 4 + 1)
                    dve.tensor_scalar(inner[:, e, :], banks[4 + (e // 4) % 4][:, (e % 4) * NG:(e % 4 + 1) * NG],
                                      b1[:, e:e + 1], 0.0, ALU.add, ALU.max).then_inc(inn, 1)
                for q in range(C1):
                    dve.wait_ge(w2d, C1 * c + q + 1)
                    for s in range(2, S_):
                        last = dve.tensor_copy(
                            res_t[:, :, :, 2 * q * S_ + s:2 * q * S_ + s + S_ + 1:S_].rearrange("p n cb e -> p e cb n"),
                            banks[4 * (q % 2) + s][:].rearrange("p (e cb n) -> p e cb n", e=2, cb=CB))
                    last.then_inc(res_dve, 1)

                def add(t):
                    if t % TT == 0:
                        dve.wait_ge(xr_loaded, 16 * (CH * c + t // TT) + 16)
                    dve.wait_ge(od, TD * c + t + 1)
                    xs = xa[:, (t // TT) % 2, t % TT, :]
                    dve.tensor_tensor(xs, xs, banks[4 + t % 2][:, 0:C], ALU.add).then_inc(fin, 1)

                for t in range(TD):
                    dve.wait_ge(rtd, TD * c + t + 1)
                    if t >= 2:
                        dve.wait_ge(od, TD * c + t - 1)
                    for a in range(2):
                        dve.tensor_tensor(res[:, t % 2, 2 * a:2 * a + 2, :],
                                          banks[2 * (t % 2) + a][:].rearrange("p (g c) -> p g c", g=2),
                                          b2[:].unsqueeze(1).to_broadcast([P, 2, C]), ALU.add).then_inc(rc, 1)
                    if t:
                        add(t - 1)
                add(TD - 1)
                dve.wait_ge(stored, 16 * CH * (c + 1))
                dve.memset(spare[:], 0.0).then_inc(chunk_free, 1)


def kernel(**inputs):
    import numpy as np
    import concourse.bacc as bacc
    from concourse.bass_utils import run_bass_kernel_spmd

    a = {n: np.asarray(v) for n, v in inputs.items()}
    f = np.float32

    def cols(v):
        return v.reshape(LAYERS, CB, P).transpose(2, 0, 1)

    def rows(v, nb):
        l, o, i = v.shape
        return v.transpose(0, 2, 1).reshape(l, nb, P, o).transpose(0, 2, 1, 3).reshape(l, P, nb * o)

    L0 = {n[8:]: v for n, v in a.items() if n.startswith("L0_attn_")}
    names = ["ln1_w", "ln1_b", "ln2_w", "ln2_b", "time_decay", "time_first", "tmk", "tmv", "tmr", "cmk", "cmr"]
    arrays = {
        "x_in": L0["x"],
        "ln0": np.stack([L0["ln0_w"], L0["ln0_b"]]),
        "par_in": np.stack([cols(L0[n]) for n in names], axis=1),
        "kvr_in": np.concatenate([rows(L0[n], CB) for n in ("Wk", "Wv", "Wr")], axis=2),
        "wo_in": rows(L0["Wo"], CB),
        "wck_in": rows(L0["Wck"], CB),
        "wcr_in": rows(L0["Wcr"], CB),
        "wcv_in": rows(L0["Wcv"], FB),
        "ident_in": np.eye(P, dtype=f),
        "wc_in": a["L0_ffn_Wc"].reshape(CB, P, ES).transpose(1, 0, 2),
        "bctie_in": np.concatenate([a["L0_ffn_bc"].reshape(ES, 1),
                                    np.broadcast_to(np.linspace(0.0, 1e-6, G, dtype=f), (ES, G))], axis=1),
        "w1_in": a["L0_ffn_W1"].reshape(E_ // OCT, OCT * S_, CB, P, EF).transpose(0, 3, 2, 1, 4).reshape(E_ // OCT, P, OCT * C),
        "b1_in": a["L0_ffn_b1"].transpose(1, 2, 0).reshape(S_ * EF, E_),
        "w2_in": a["L0_ffn_W2"].reshape(E_ // OCT, OCT, S_, C, EF).transpose(0, 2, 4, 1, 3).reshape(E_ // OCT, P, OCT * C),
        "b2_in": a["L0_ffn_b2"].reshape(ES, C),
    }
    nc = bacc.Bacc("TRN2", target_bir_lowering=False, num_devices=1)
    args = {}
    for n, v in arrays.items():
        arrays[n] = v = np.ascontiguousarray(v)
        args[n] = nc.dram_tensor(n, v.shape, mybir.dt.from_np(v.dtype), kind="ExternalInput").ap()
    args["out"] = nc.dram_tensor("out", (SEQS, T, C), F32, kind="ExternalOutput").ap()
    rwkv_moe(nc, **args)
    r = run_bass_kernel_spmd(nc, [arrays], core_ids=[0])
    return r.results[0]["out"]
```

```python
import concourse.bass as bass
from concourse import mybir
from contextlib import ExitStack

F32 = mybir.dt.float32
F32R = mybir.dt.float32r
ALU = mybir.AluOpType
ACT = mybir.ActivationFunctionType
AX = mybir.AxisListType

P = 128
SEQS, T, C, F = 16, 512, 256, 1024
LAYERS = 4
CB, FB, TT = C // P, F // P, T // P
STEPS = LAYERS * SEQS
EPS = 1e-5
NEG = -1e38
(LN1W, LN1B, LN2W, LN2B, DECAY, FIRST, TMK, TMV, TMR, CMK, CMR) = range(11)
NPAR = 11

SLOTS = 5

PASSES = ((0, 0), (0, 1), (1, 0))

G = 32
E_, S_, EF = 32, 4, 32
ES = E_ * S_
CHUNKS = 2
CH = SEQS // CHUNKS
NG = CH * T // G
GT = P // G
OCT = 8


def later(count):
    return not isinstance(count, int) or count > 0


def held(dve, spare, sem, count):
    dve.wait_ge(sem, count)
    dve.memset(spare, 0.0)


def rwkv_moe(nc, x_in, ln0, par_in, kvr_in, wo_in, wck_in, wcr_in, wcv_in, ident_in,
             wc_in, bctie_in, w1_in, b1_in, w2_in, b2_in, out):
    outer = ExitStack()
    with outer:
        ident = outer.enter_context(nc.sbuf_tensor("ident", [P, P], F32))
        eps_pow = outer.enter_context(nc.sbuf_tensor("eps_pow", [P, TT], F32))
        x_mem = nc.dram_tensor("x_mem", (SEQS, T, C), F32, kind="Internal").ap()
        layers(nc, ident, eps_pow, x_mem, x_in, ln0, ident_in, par_in, kvr_in, wo_in, wck_in, wcr_in, wcv_in)
        experts(nc, ident, eps_pow, x_mem, x_in, wc_in, bctie_in, w1_in, b1_in, w2_in, b2_in, out)


def layers(nc, ident, eps_pow, x_mem, x_in, ln0, ident_in, par_in, kvr_in, wo_in, wck_in, wcr_in, wcv_in):
    ctx = ExitStack()
    with ctx:
        def sb(name, shape):
            return ctx.enter_context(nc.sbuf_tensor(name, shape, F32))

        def halves(name, shape):
            return [ctx.enter_context(nc.sbuf_tensor(name + end, shape, F32R)) for end in ("_hi", "_lo")]

        def sem(name):
            return ctx.enter_context(nc.semaphore(name))

        U = [P, CB, T]
        x = sb("x", [P, SLOTS, TT, C])
        spare = sb("spare", [P, 1])
        ln0_sb = sb("ln0_sb", [P, 2, C])
        par = sb("par", [P, NPAR, LAYERS, CB])
        kvr_w = halves("kvr_w", [P, 3, CB, C])
        wo_w = sb("wo_w", [P, CB, C])
        wck_w = halves("wck_w", [P, CB, F])
        wcr_w = sb("wcr_w", [P, CB, C])
        wcv_w = halves("wcv_w", [P, FB, C])
        whole = sb("whole", [P, 2, TT * C])

        kvr_whole = whole[:].rearrange("p a b -> p (a b)")[:, 0:3 * CB * C]

        st = [sb(f"st{a}", [P, TT, 6]) for a in range(4)]
        mv = [sb(f"mv{a}", [P, TT, 2]) for a in range(4)]
        ve = [sb(f"ve{a}", [P, TT]) for a in range(4)]
        rstd = [sb(f"rstd{a}", [P, TT]) for a in range(4)]
        xd = [sb(f"xd{a}", U) for a in range(2)]
        h = [sb(f"h{a}", [P, CB, T + 1]) for a in range(2)]
        kvr_x = [halves(f"kvr_x{a}", U) for a in range(3)]
        xr2 = xd[1]
        xk2h, kf = halves("xk2", U), halves("kf", [P, FB, T])
        th2 = sb("th2", [P, TT * C])
        k_sb, v_sb = sb("k_sb", U), sb("v_sb", U)
        th = k_sb
        num = v_sb
        pp = sb("pp", [P, CB, T + 1])
        aa = sb("aa", [P, CB, T + 1])
        bb = sb("bb", [P, CB, T + 1])
        e1b, e2b = sb("e1b", U), sb("e2b", U)
        nd = sb("nd", U)
        e12 = sb("e12", [P, 2, CB, T])
        rw = sb("rw", U)
        xk2 = rw
        xkvr = nd, e1b, xd[0]

        pairs = [ctx.enter_context(nc.psum_tensor(f"pair{a}", [P, 2, 512], F32)) for a in range(4)]

        const_loaded, const_set = sem("const_loaded"), sem("const_set")
        par_loaded, par_exp, par_ready = sem("par_loaded"), sem("par_exp"), sem("par_ready")
        edges = sem("edges")
        x_loaded, x_stored = sem("x_loaded"), sem("x_stored")
        kvr_staged, wo_loaded, cr_loaded = sem("kvr_staged"), sem("wo_loaded"), sem("cr_loaded")
        stats = [sem(f"stats{a}") for a in range(4)]
        aggr = [sem(f"aggr{a}") for a in range(4)]
        var = [sem(f"var{a}") for a in range(4)]
        rs = [sem(f"rstd{a}_ready") for a in range(4)]
        xn = [sem(f"xn{a}") for a in range(4)]
        scaled, x_first = sem("scaled"), sem("x_first")
        tr = [sem("tr1"), sem("tr2")]
        hs = [sem("h1_ready"), sem("h2_ready")]
        ds_ = [sem("d1_ready"), sem("d2_ready")]
        mixed1, mixed2 = sem("mixed1"), sem("mixed2")
        k_done, v_done, r_done = sem("k_done"), sem("v_done"), sem("r_done")
        k_copied, v_copied, th_ready = sem("k_copied"), sem("v_copied"), sem("th_ready")
        pp_ready, e1_arg, e2_arg = sem("pp_ready"), sem("e1_arg"), sem("e2_arg")
        nd_ready, e12_arg, e12_ready = sem("nd_ready"), sem("e12_arg"), sem("e12_ready")
        e1b_ready, e2b_ready, ev_ready = sem("e1b_ready"), sem("e2b_ready"), sem("ev_ready")
        states = sem("states")
        m1_ready, m2_ready, m3_ready = sem("m1_ready"), sem("m2_ready"), sem("m3_ready")
        num_ready, den_ready, ln_ready, rden_ready = sem("num_ready"), sem("den_ready"), sem("ln_ready"), sem("rden_ready")
        gated, rw_ready = sem("gated"), sem("rw_ready")
        wo_done, x_mid = sem("wo_done"), sem("x_mid")
        cr_done, th2_ready = sem("cr_done"), sem("th2_ready")
        ck_done, relu_done, squared, kf_hi, kf_lo = sem("ck_done"), sem("relu_done"), sem("squared"), sem("kf_hi"), sem("kf_lo")
        xk2_hi, xk2_lo = sem("xk2_hi"), sem("xk2_lo")
        x_hi = [sem(f"x{a}_hi") for a in "kvr"]
        x_lo = [sem(f"x{a}_lo") for a in "kvr"]
        kvr_hi, kvr_lo = sem("kvr_hi"), sem("kvr_lo")
        w_staged, w_hi, w_lo = sem("w_staged"), sem("w_hi"), sem("w_lo")
        cv_done, gated2, x_done = sem("cv_done"), sem("gated2"), sem("x_done")
        block = ctx.enter_context(nc.Block())

        def inside(n):
            return not isinstance(n, int) or 0 <= n < STEPS

        def pipeline(engine, step):
            step(0, True)
            step(1, True, wide=0)
            step(2, True)
            with engine.Fori(3, SEQS - 2) as i:
                step(i, True)
            step(SEQS - 2, False)
            step(SEQS - 1, False, kvr=1)
            step(SEQS, False)
            with engine.Fori(1, LAYERS - 1) as l:
                step(SEQS * l + 1, False, wide=l)
                with engine.Fori(2, SEQS - 1) as s:
                    step(SEQS * l + s, False)
                step(SEQS * l + SEQS - 1, False, kvr=l + 1)
                step(SEQS * l + SEQS, False)
            step(STEPS - SEQS + 1, False, wide=LAYERS - 1)
            with engine.Fori(STEPS - SEQS + 2, STEPS - 2) as i:
                step(i, False)
            for i in range(STEPS - 2, STEPS + 2):
                step(i, False)

        def slot(n):
            return x[:, bass.ds(n % SLOTS, 1), :, :].rearrange("p s t c -> p (s t) c")

        def col(which, n, cb):
            return par[:, which, bass.ds(n // SEQS, 1), cb]

        @block.sync
        def _(sp):
            def rows(mem, n):
                return mem[bass.ds(n % SEQS, 1)].rearrange("s (t p) c -> p (s t) c", p=P)

            def load(n, mem):
                if later(n):
                    sp.wait_ge(x_loaded, 16 * n)
                sp.dma_start(slot(n), rows(mem, n)).then_inc(x_loaded, 16)

            def weights(mem, l):
                return mem[bass.ds(l, 1)].rearrange("l p n -> (l p) n")

            def step(i, first, wide=None, kvr=None):
                if kvr is not None:
                    sp.wait_ge(kf_hi, 4 * SEQS * kvr - 8)
                    sp.wait_ge(kf_lo, 4 * SEQS * kvr - 8)
                    stage_kvr(kvr)
                if wide is not None and later(wide):
                    sp.wait_ge(kf_hi, 4 * SEQS * wide)
                    sp.wait_ge(kf_lo, 4 * SEQS * wide)
                if wide is not None:
                    if not later(wide):
                        sp.wait_ge(kvr_lo, 1)
                    sp.dma_start(whole[:].rearrange("p a b -> p (a b)"), weights(wck_in, wide)).then_inc(w_staged, 16)
                if inside(i + 2):
                    if inside(i - 3):
                        sp.wait_ge(x_stored, 16 * i - 32)
                    load(i + 2, x_in if first else x_mem)
                if wide is not None:
                    sp.wait_ge(w_hi, 2 * wide + 1)
                    sp.wait_ge(w_lo, 2 * wide + 1)
                    sp.dma_start(whole[:].rearrange("p a b -> p (a b)"), weights(wcv_in, wide)).then_inc(w_staged, 16)
                if inside(i - 2):
                    sp.wait_ge(x_done, i - 1)
                    if inside(i - 3):
                        sp.wait_ge(x_stored, 16 * i - 32)
                    sp.dma_start(rows(x_mem, i - 2), slot(i - 2)).then_inc(x_stored, 16)

            def stage_kvr(l):
                sp.dma_start(kvr_whole, weights(kvr_in, l)).then_inc(kvr_staged, 16)

            def out_weights(l):
                if later(l):
                    sp.wait_ge(wo_done, SEQS * l)
                sp.dma_start(wo_w[:].rearrange("p b c -> p (b c)"), weights(wo_in, l)).then_inc(wo_loaded, 16)

            def gate_weights(l):
                if later(l):
                    sp.wait_ge(cr_done, SEQS * l)
                sp.dma_start(wcr_w[:].rearrange("p b c -> p (b c)"), weights(wcr_in, l)).then_inc(cr_loaded, 16)

            sp.dma_start(par[:], par_in).then_inc(par_loaded, 16)
            sp.dma_start(ln0_sb[:], ln0.unsqueeze(0).to_broadcast([P, 2, C])).then_inc(const_loaded, 16)
            sp.dma_start(ident[:], ident_in).then_inc(const_loaded, 16)
            load(0, x_in)
            load(1, x_in)
            stage_kvr(0)
            out_weights(0)
            gate_weights(0)
            step(0, True)
            step(1, True, wide=0)
            step(2, True)
            with sp.Fori(3, SEQS - 2) as i:
                step(i, True)
            step(SEQS - 2, False)
            step(SEQS - 1, False, kvr=1)
            with sp.Fori(1, LAYERS - 1) as l:
                out_weights(l)
                step(SEQS * l, False)
                gate_weights(l)
                step(SEQS * l + 1, False, wide=l)
                with sp.Fori(2, SEQS - 2) as s:
                    step(SEQS * l + s, False)
                step(SEQS * l + SEQS - 2, False)
                step(SEQS * l + SEQS - 1, False, kvr=l + 1)
            out_weights(LAYERS - 1)
            step(STEPS - SEQS, False)
            gate_weights(LAYERS - 1)
            step(STEPS - SEQS + 1, False, wide=LAYERS - 1)
            with sp.Fori(STEPS - SEQS + 2, STEPS - 2) as i:
                step(i, False)
            for i in range(STEPS - 2, STEPS + 2):
                step(i, False)
            sp.wait_ge(x_stored, 16 * STEPS)

        @block.tensor
        def _(pe):
            def kvr_of(k):
                return [half[:, k] for half in kvr_w]

            def channel_major_split(pair, w, inp, blocks, done):
                for j, m in enumerate(blocks):
                    for cb in range(CB):
                        for a, b in PASSES:
                            last = pe.matmul(pair[:, j, :], w[a][:, cb, m * P:(m + 1) * P], inp[b][:, cb, :],
                                             start=cb == 0 and a + b == 0, stop=cb == CB - 1 and (a, b) == PASSES[-1])
                last.then_inc(done, 1)

            def token_major_split(pair, inp, w, nb, tiles, done=None):
                for t in tiles:
                    for k in range(nb):
                        for a, b in PASSES:
                            last = pe.matmul(pair[:, t // 2, (t % 2) * C:(t % 2 + 1) * C], inp[a][:, k, t * P:(t + 1) * P],
                                             w[b][:, k, :], start=k == 0 and a + b == 0, stop=k == nb - 1 and (a, b) == PASSES[-1])
                if done is not None:
                    last.then_inc(done, 1)

            def token_major(pair, inp, w, nb, done):
                for t in range(TT):
                    for b in range(nb):
                        last = pe.matmul(pair[:, t // 2, (t % 2) * C:(t % 2 + 1) * C], inp[:, b, t * P:(t + 1) * P],
                                         w[:, b, :], start=b == 0, stop=b == nb - 1)
                last.then_inc(done, 1)

            def transposes(pair, a, n):
                pe.wait_ge(xn[a], n + 1)
                xt = xd[a][:].rearrange("p a b -> p (a b)").rearrange("p (t c) -> p t c", t=TT)
                for cb in range(CB):
                    for t in range(TT):
                        last = pe.transpose(pair[:, cb, t * P:(t + 1) * P], xt[:, t, cb * P:(cb + 1) * P], ident[:])
                last.then_inc(tr[a], 1)

            def step(i, first, wide=None, kvr=None):
                now, prev, old, nxt = inside(i), inside(i - 1), inside(i - 2), inside(i + 1)
                if now:
                    pe.wait_ge(kvr_lo, i // SEQS + 1)
                    if inside(i - 2):
                        pe.wait_ge(relu_done, 4 * (i - 2) + 2)
                    elif prev:
                        pe.wait_ge(th_ready, i)
                    pe.wait_ge(x_lo[0], i + 1)
                    channel_major_split(pairs[0], kvr_of(0), kvr_x[0], range(CB), k_done)
                    if inside(i - 2):
                        pe.wait_ge(relu_done, 4 * (i - 2) + 3)
                    pe.wait_ge(x_lo[1], i + 1)
                    channel_major_split(pairs[1], kvr_of(1), kvr_x[1], range(CB), v_done)
                if old:
                    pe.wait_ge(w_lo, 2 * ((i - 2) // SEQS) + 2)
                    pe.wait_ge(kf_hi, 4 * (i - 2) + 4)
                    pe.wait_ge(kf_lo, 4 * (i - 2) + 4)
                    if inside(i - 1):
                        pe.wait_ge(x_mid, i)
                    token_major_split(pairs[3], kf, wcv_w, FB, (0,))
                if prev:
                    if inside(i - 2):
                        pe.wait_ge(relu_done, 4 * (i - 2) + 4)
                    transposes(pairs[2], 1, i - 1)
                if old:
                    token_major_split(pairs[3], kf, wcv_w, FB, range(1, TT), cv_done)
                if now:
                    pe.wait_ge(k_copied, i + 1)
                    pe.wait_ge(x_lo[2], i + 1)
                    channel_major_split(pairs[0], kvr_of(2), kvr_x[2], range(CB), r_done)
                if nxt:
                    if now:
                        pe.wait_ge(v_copied, i + 1)
                    transposes(pairs[1], 0, i + 1)
                if prev:
                    pe.wait_ge(cr_loaded, 16 * ((i - 1) // SEQS) + 16)
                    pe.wait_ge(mixed2, 2 * i)
                    pe.wait_ge(hs[1], i)
                    token_major(pairs[2], xr2, wcr_w, CB, cr_done)
                    pe.wait_ge(w_lo, 2 * ((i - 1) // SEQS) + 1)
                    pe.wait_ge(xk2_hi, i)
                    pe.wait_ge(xk2_lo, i)
                    if old:
                        pe.wait_ge(gated2, i - 1)
                    channel_major_split(pairs[3], wck_w, xk2h, (0, 1), ck_done)
                    if now:
                        pe.wait_ge(th_ready, i + 1)
                    channel_major_split(pairs[0], wck_w, xk2h, (2, 3), ck_done)
                    if nxt:
                        pe.wait_ge(hs[0], i + 2)
                    channel_major_split(pairs[1], wck_w, xk2h, (4, 5), ck_done)
                    pe.wait_ge(th2_ready, i)
                    channel_major_split(pairs[2], wck_w, xk2h, (6, 7), ck_done)
                if now:
                    pe.wait_ge(wo_loaded, 16 * (i // SEQS) + 16)
                    if prev:
                        pe.wait_ge(relu_done, 4 * (i - 1) + 1)
                    pe.wait_ge(rw_ready, i + 1)
                    token_major(pairs[3], rw, wo_w, CB, wo_done)

            pe.wait_ge(const_loaded, 32)
            transposes(pairs[1], 0, 0)
            pipeline(pe, step)

        @block.scalar
        def _(act):
            def affine(pair, a, n, ready):
                act.wait_ge(tr[a], n + 1)
                if later(n):
                    if a:
                        act.wait_ge(mixed2, 2 * n)
                    else:
                        act.wait_ge(mixed1, 3 * n)
                wi, bi = (LN2W, LN2B) if a else (LN1W, LN1B)
                for cb in range(CB):
                    last = act.activation(h[a][:, cb, 1:], pair[:, cb, :], ACT.Identity,
                                          bias=col(bi, n, cb), scale=col(wi, n, cb))
                last.then_inc(ready, 1)

            def relu(m, j, wide, kvr):
                act.wait_ge(ck_done, 4 * m + j + 1)
                if j >= 2 or later(m):
                    act.wait_ge(kf_lo, 4 * m + j - 1)
                if wide is not None and not j:
                    act.wait_ge(w_lo, 2 * wide + 2)
                if kvr is not None and not j:
                    act.wait_ge(kvr_lo, kvr + 1)
                act.activation(whole[:, j % 2, :], pairs[(j + 3) % 4][:].rearrange("p a b -> p (a b)"),
                               ACT.Relu).then_inc(relu_done, 1)

            def kf_high(m, j):
                act.wait_ge(squared, 4 * m + j + 1)
                if not j and later(m):
                    act.wait_ge(cv_done, m)
                act.activation(kf[0][:, 2 * j:2 * j + 2, :].rearrange("p a b -> p (a b)"), whole[:, j % 2, :],
                               ACT.Identity).then_inc(kf_hi, 1)

            def kvr_high(l):
                act.wait_ge(kvr_staged, 16 * l + 16)
                if later(l):
                    act.wait_ge(r_done, SEQS * l)
                act.activation(kvr_w[0][:].rearrange("p a b c -> p (a b c)"), kvr_whole, ACT.Identity).then_inc(kvr_hi, 1)

            def x_high(a, n):
                act.wait_ge(mixed1, 3 * n + a + 1)
                if later(n):
                    act.wait_ge((k_done, v_done, r_done)[a], n)
                act.activation(kvr_x[a][0][:], xkvr[a][:], ACT.Identity).then_inc(x_hi[a], 1)

            def weights_high(w, k, l, used):
                act.wait_ge(w_staged, 32 * l + 16 * k + 16)
                if later(l):
                    act.wait_ge(used, (SEQS if k else 4 * SEQS) * l)
                act.activation(w[0][:].rearrange("p a b -> p (a b)"), whole[:].rearrange("p a b -> p (a b)"),
                               ACT.Identity).then_inc(w_hi, 1)

            def step(i, first, wide=None, kvr=None):
                now, prev, nxt = inside(i), inside(i - 1), inside(i + 1)
                if now:
                    act.wait_ge(k_done, i + 1)
                    if prev:
                        act.wait_ge(rw_ready, i)
                    act.activation(k_sb[:], pairs[0][:], ACT.Identity).then_inc(k_copied, 1)
                    act.wait_ge(v_done, i + 1)
                    act.activation(v_sb[:], pairs[1][:], ACT.Identity).then_inc(v_copied, 1)
                if prev:
                    affine(pairs[2], 1, i - 1, hs[1])
                if now:
                    act.wait_ge(e1_arg, i + 1)
                    for cb in range(CB):
                        last = act.activation(e1b[:, cb, :], e1b[:, cb, :], ACT.Exp, bias=col(DECAY, i, cb))
                    last.then_inc(e1b_ready, 1)
                    act.wait_ge(e2_arg, i + 1)
                    act.activation(e2b[:], e2b[:], ACT.Exp).then_inc(e2b_ready, 1)
                    act.wait_ge(e12_arg, 2 * i + 2)
                    act.activation(e12[:], e12[:], ACT.Exp).then_inc(e12_ready, 1)
                if wide is not None:
                    weights_high(wck_w, 0, wide, ck_done)
                if prev:
                    act.wait_ge(mixed2, 2 * i - 1)
                    if later(i - 1):
                        act.wait_ge(ck_done, 4 * i - 4)
                    act.activation(xk2h[0][:], xk2[:], ACT.Identity).then_inc(xk2_hi, 1)
                if now:
                    act.wait_ge(r_done, i + 1)
                    act.activation(th[:], pairs[0][:], ACT.Tanh, scale=0.5).then_inc(th_ready, 1)
                if wide is not None:
                    weights_high(wcv_w, 1, wide, cv_done)
                if kvr is not None:
                    kvr_high(kvr)
                if nxt:
                    affine(pairs[1], 0, i + 1, hs[0])
                if now:
                    act.wait_ge(den_ready, i + 1)
                    den = e12[:, 0]
                    act.activation(den, den, ACT.Ln).then_inc(ln_ready, 1)
                    act.wait_ge(ln_ready, i + 1)
                    act.activation(den, den, ACT.Exp, scale=-1.0).then_inc(rden_ready, 1)
                if nxt:
                    x_high(0, i + 1)
                if prev:
                    relu(i - 1, 0, wide, kvr)
                    act.wait_ge(cr_done, i)
                    if inside(i - 2):
                        act.wait_ge(x_done, i - 1)
                    act.activation(th2[:],
                                   pairs[2][:].rearrange("p a b -> p (a b)"), ACT.Tanh, scale=0.5).then_inc(th2_ready, 1)
                if prev:
                    relu(i - 1, 1, wide, kvr)
                    kf_high(i - 1, 0)
                    kf_high(i - 1, 1)
                if nxt:
                    x_high(1, i + 1)
                if prev:
                    relu(i - 1, 2, wide, kvr)
                    relu(i - 1, 3, wide, kvr)
                    kf_high(i - 1, 2)
                    kf_high(i - 1, 3)
                if nxt:
                    x_high(2, i + 1)

            act.wait_ge(par_loaded, 16)
            act.activation(par[:, DECAY], par[:, DECAY], ACT.Exp).then_inc(par_exp, 1)
            act.wait_ge(par_ready, 1)
            act.wait_ge(edges, 5)
            kvr_high(0)
            affine(pairs[1], 0, 0, hs[0])
            for a in range(3):
                x_high(a, 0)
            pipeline(act, step)

        @block.gpsimd
        def _(pool):
            def power(a, n):
                pool.wait_ge(var[a], n + 1)
                pool.tensor_tensor(rstd[a][:], ve[a][:], eps_pow[:], ALU.pow).then_inc(rs[a], 1)

            def x_low(a, n):
                pool.wait_ge(x_hi[a], n + 1)
                pool.tensor_tensor(kvr_x[a][1][:], xkvr[a][:], kvr_x[a][0][:], ALU.subtract).then_inc(x_lo[a], 1)

            def diff(a, n):
                pool.wait_ge(hs[a], n + 1)
                pool.tensor_tensor(xd[a][:], h[a][:, :, 1:], h[a][:, :, 0:T], ALU.subtract).then_inc(ds_[a], 1)

            def kf_low(m, j):
                pool.wait_ge(kf_hi, 4 * m + j + 1)
                pool.tensor_tensor(kf[1][:, 2 * j:2 * j + 2, :].rearrange("p a b -> p (a b)"), whole[:, j % 2, :],
                                   kf[0][:, 2 * j:2 * j + 2, :].rearrange("p a b -> p (a b)"),
                                   ALU.subtract).then_inc(kf_lo, 1)

            def step(i, first, wide=None, kvr=None):
                if inside(i - 1):
                    power(1, i - 1)
                if inside(i):
                    pool.wait_ge(pp_ready, i + 1)
                    pool.wait_ge(x_lo[1], i + 1)
                    pool.tensor_tensor(e1b[:], pp[:, :, 0:T], pp[:, :, 1:], ALU.subtract).then_inc(e1_arg, 1)
                    pool.tensor_tensor(e2b[:], k_sb[:], pp[:, :, 1:], ALU.subtract).then_inc(e2_arg, 1)
                if inside(i + 1):
                    power(0, i + 1)
                if inside(i - 1):
                    diff(1, i - 1)
                if inside(i):
                    pool.wait_ge(e2b_ready, i + 1)
                    pool.wait_ge(v_copied, i + 1)
                    pool.wait_ge(e12_arg, 2 * i + 2)
                    pool.tensor_tensor(nd[:], e2b[:], v_sb[:], ALU.mult).then_inc(ev_ready, 1)
                    pool.wait_ge(e12_ready, i + 1)
                    pool.tensor_tensor(v_sb[:], v_sb[:], e12[:, 1], ALU.mult).then_inc(m2_ready, 1)
                if inside(i - 1):
                    pool.wait_ge(xk2_hi, i)
                    pool.tensor_tensor(xk2h[1][:], xk2[:], xk2h[0][:], ALU.subtract).then_inc(xk2_lo, 1)
                if inside(i + 1):
                    diff(0, i + 1)
                if first:
                    power(2, i + 2)
                if inside(i + 1):
                    x_low(0, i + 1)
                if first:
                    power(3, i + 2)
                if inside(i - 1):
                    kf_low(i - 1, 0)
                    kf_low(i - 1, 1)
                if inside(i + 1):
                    x_low(1, i + 1)
                if inside(i - 1):
                    kf_low(i - 1, 2)
                    kf_low(i - 1, 3)

            pool.memset(eps_pow[:], -0.5).then_inc(const_set, 1)
            pool.wait_ge(const_set, 1)
            for n in range(2):
                power(2, n)
                power(3, n)
            power(0, 0)
            diff(0, 0)
            x_low(0, 0)
            x_low(1, 0)
            pipeline(pool, step)

        @block.vector
        def _(dve):
            def norm_stats(a, n):
                for t in range(TT):
                    last = dve.bn_stats(st[a][:, t, :], slot(n)[:, t, :])
                last.then_inc(stats[a], 1)
                held(dve, spare[:], stats[a], n + 1)
                for t in range(TT):
                    last = dve.bn_aggr(mv[a][:, t, :], st[a][:, t, :])
                last.then_inc(aggr[a], 1)
                dve.wait_ge(aggr[a], n + 1)
                dve.tensor_scalar(ve[a][:], mv[a][:, :, 1], EPS, None, ALU.add).then_inc(var[a], 1)

            def normalise(a, n, dst):
                dve.wait_ge(rs[a], n + 1)
                for t in range(TT):
                    last = dve.tensor_scalar(dst[:, t, :], slot(n)[:, t, :], mv[a][:, t, 0:1], rstd[a][:, t:t + 1],
                                             ALU.subtract, ALU.mult)
                last.then_inc(xn[a], 1)

            def rows(a):
                return xd[a][:].rearrange("p a b -> p (a b)").rearrange("p (t c) -> p t c", t=TT)

            def first_stats(n):
                held(dve, spare[:], x_loaded, 16 * n + 16)
                norm_stats(2, n)

            def first_norm(n):
                normalise(2, n, slot(n))
                held(dve, spare[:], xn[2], n + 1)
                norm_stats(3, n)

            def second_norm(n):
                normalise(3, n, slot(n))
                dve.wait_ge(xn[3], n + 1)
                dve.tensor_tensor(slot(n), slot(n), ln0_sb[:, 0:1, :].to_broadcast([P, TT, C]), ALU.mult).then_inc(scaled, 1)
                dve.wait_ge(scaled, n + 1)
                dve.tensor_tensor(slot(n), slot(n), ln0_sb[:, 1:2, :].to_broadcast([P, TT, C]), ALU.add).then_inc(x_first, 1)

            def mix(dst, a, which, n, ready):
                for cb in range(CB):
                    last = dve.scalar_tensor_tensor(dst[:, cb, :], xd[a][:, cb, :], col(which, n, cb), h[a][:, cb, 0:T],
                                                    ALU.mult, ALU.add)
                last.then_inc(ready, 1)

            def mix_k(n):
                dve.wait_ge(ds_[0], n + 1)
                mix(xkvr[0], 0, TMK, n, mixed1)

            def mix_vr(n):
                mix(xkvr[1], 0, TMV, n, mixed1)
                mix(xkvr[2], 0, TMR, n, mixed1)

            def kvr_low(l):
                dve.wait_ge(kvr_hi, l + 1)
                dve.tensor_tensor(kvr_w[1][:].rearrange("p a b c -> p (a b c)"), kvr_whole,
                                  kvr_w[0][:].rearrange("p a b c -> p (a b c)"), ALU.subtract).then_inc(kvr_lo, 1)

            def weights_low(w, k, l):
                dve.wait_ge(w_hi, 2 * l + k + 1)
                dve.tensor_tensor(w[1][:].rearrange("p a b -> p (a b)"), whole[:].rearrange("p a b -> p (a b)"),
                                  w[0][:].rearrange("p a b -> p (a b)"), ALU.subtract).then_inc(w_lo, 1)

            def square(m, j):
                dve.wait_ge(relu_done, 4 * m + j + 1)
                dve.tensor_tensor(whole[:, j % 2, :], whole[:, j % 2, :], whole[:, j % 2, :], ALU.mult).then_inc(squared, 1)

            def step(i, first, wide=None, kvr=None):
                now, prev, old, nxt = inside(i), inside(i - 1), inside(i - 2), inside(i + 1)
                if prev:
                    xs = slot(i - 1)
                    dve.wait_ge(wo_done, i)
                    pair = pairs[3][:].rearrange("p a (b c) -> p (a b) c", c=C)
                    dve.scalar_tensor_tensor(xs, pair, 0.5, xs, ALU.mult, ALU.add).then_inc(x_mid, 1)
                if old:
                    square(i - 2, 3)
                if prev:
                    held(dve, spare[:], x_mid, i)
                    norm_stats(1, i - 1)
                if now:
                    dve.wait_ge(k_copied, i + 1)
                    for cb in range(CB):
                        last = dve.tensor_tensor_scan(pp[:, cb, 1:], col(DECAY, i, cb).to_broadcast([P, T]), k_sb[:, cb, :],
                                                      NEG, ALU.add, ALU.max)
                    last.then_inc(pp_ready, 1)
                if prev:
                    if inside(i - 2):
                        dve.wait_ge(cr_done, i - 1)
                    normalise(1, i - 1, rows(1))
                if now:
                    dve.wait_ge(pp_ready, i + 1)
                    dve.wait_ge(x_lo[0], i + 1)
                    for cb in range(CB):
                        last = dve.scalar_tensor_tensor(nd[:, cb, :], k_sb[:, cb, :], col(FIRST, i, cb), pp[:, cb, 0:T],
                                                        ALU.add, ALU.subtract)
                    last.then_inc(nd_ready, 1)
                if nxt:
                    if not first:
                        held(dve, spare[:], x_loaded, 16 * (i + 1) + 16)
                    else:
                        held(dve, spare[:], x_first, i + 2)
                    norm_stats(0, i + 1)
                if now:
                    dve.wait_ge(nd_ready, i + 1)
                    dve.tensor_scalar(e12[:, 0], nd[:], -1.0, 0.0, ALU.mult, ALU.min).then_inc(e12_arg, 1)
                    dve.tensor_scalar(e12[:, 1], nd[:], 0.0, None, ALU.min).then_inc(e12_arg, 1)
                if now:
                    dve.wait_ge(x_hi[2], i + 1)
                    dve.tensor_tensor(kvr_x[2][1][:], xkvr[2][:], kvr_x[2][0][:], ALU.subtract).then_inc(x_lo[2], 1)
                if nxt:
                    if now:
                        dve.wait_ge(x_lo[2], i + 1)
                    normalise(0, i + 1, rows(0))
                if wide is not None:
                    weights_low(wck_w, 0, wide)
                if prev:
                    dve.wait_ge(ds_[1], i)
                    mix(xk2, 1, CMK, i - 1, mixed2)
                    mix(xr2, 1, CMR, i - 1, mixed2)
                if now:
                    dve.wait_ge(e1b_ready, i + 1)
                    dve.wait_ge(e2b_ready, i + 1)
                    for cb in range(CB):
                        last = dve.tensor_tensor_scan(bb[:, cb, 1:], e1b[:, cb, :], e2b[:, cb, :], 0.0, ALU.mult, ALU.add)
                    last.then_inc(states, 1)
                    dve.wait_ge(ev_ready, i + 1)
                    for cb in range(CB):
                        last = dve.tensor_tensor_scan(aa[:, cb, 1:], e1b[:, cb, :], nd[:, cb, :], 0.0, ALU.mult, ALU.add)
                    last.then_inc(states, 1)
                if old:
                    dve.wait_ge(cv_done, i - 1)
                    dve.wait_ge(th2_ready, i - 1)
                    t2 = th2[:].rearrange("p (t c) -> p t c", t=TT)
                    pair = pairs[3][:].rearrange("p a (b c) -> p (a b) c", c=C)
                    dve.scalar_tensor_tensor(t2, t2, 1.0, pair, ALU.add, ALU.mult).then_inc(gated2, 1)
                if now:
                    dve.wait_ge(e12_ready, i + 1)
                    dve.wait_ge(states, 2 * i + 2)
                    dve.tensor_tensor(aa[:, :, 0:T], aa[:, :, 0:T], e12[:, 0], ALU.mult).then_inc(m1_ready, 1)
                    dve.tensor_tensor(e12[:, 0], bb[:, :, 0:T], e12[:, 0], ALU.mult).then_inc(m3_ready, 1)
                    dve.wait_ge(m1_ready, i + 1)
                    dve.wait_ge(m2_ready, i + 1)
                    dve.tensor_tensor(num[:], aa[:, :, 0:T], v_sb[:], ALU.add).then_inc(num_ready, 1)
                    dve.wait_ge(m3_ready, i + 1)
                    dve.tensor_tensor(e12[:, 0], e12[:, 0], e12[:, 1], ALU.add).then_inc(den_ready, 1)
                if wide is not None:
                    weights_low(wcv_w, 1, wide)
                if kvr is not None:
                    kvr_low(kvr)
                if first:
                    first_stats(i + 2)
                if nxt:
                    mix_k(i + 1)
                if old:
                    xs = slot(i - 2)
                    dve.wait_ge(gated2, i - 1)
                    dve.scalar_tensor_tensor(xs, t2, 0.5, xs, ALU.mult, ALU.add).then_inc(x_done, 1)
                if now:
                    dve.wait_ge(th_ready, i + 1)
                    dve.wait_ge(num_ready, i + 1)
                    dve.scalar_tensor_tensor(num[:], th[:], 1.0, num[:], ALU.add, ALU.mult).then_inc(gated, 1)
                if first:
                    first_norm(i + 2)
                if prev:
                    square(i - 1, 0)
                if now:
                    dve.wait_ge(rden_ready, i + 1)
                    dve.wait_ge(gated, i + 1)
                    if prev:
                        dve.wait_ge(xk2_lo, i)
                    dve.tensor_tensor(rw[:], num[:], e12[:, 0], ALU.mult).then_inc(rw_ready, 1)
                if prev:
                    square(i - 1, 1)
                if nxt:
                    mix_vr(i + 1)
                if prev:
                    square(i - 1, 2)
                if first:
                    second_norm(i + 2)

            for a in range(2):
                dve.memset(h[a][:, :, 0:1], 0.0).then_inc(edges, 1)
            dve.memset(pp[:, :, 0:1], NEG).then_inc(edges, 1)
            dve.memset(aa[:, :, 0:1], 0.0).then_inc(edges, 1)
            dve.memset(bb[:, :, 0:1], 0.0).then_inc(edges, 1)
            dve.wait_ge(par_exp, 1)
            dve.tensor_scalar(par[:, DECAY], par[:, DECAY], -1.0, None, ALU.mult).then_inc(par_ready, 1)
            dve.wait_ge(const_loaded, 32)
            for n in range(2):
                first_stats(n)
                first_norm(n)
                second_norm(n)
            held(dve, spare[:], x_first, 1)
            norm_stats(0, 0)
            normalise(0, 0, rows(0))
            kvr_low(0)
            mix_k(0)
            mix_vr(0)
            pipeline(dve, step)


def experts(nc, ident, eps_pow, x_mem, x_in, wc_in, bctie_in, w1_in, b1_in, w2_in, b2_in, out):
    ROWS = E_ * NG // (TT * C)
    SPREAD = 2 * TT * C // (S_ * NG)
    ctx = ExitStack()
    with ctx:
        def sb(name, shape):
            return ctx.enter_context(nc.sbuf_tensor(name, shape, F32))

        def sem(name):
            return ctx.enter_context(nc.semaphore(name))

        spare = sb("spare_e", [P, 1])
        wc = sb("wc", [P, CB, ES])
        bct = sb("bct", [P, 1 + G])
        b1 = sb("b1", [P, E_])
        b2 = sb("b2", [P, C])
        st, mv = sb("st_e", [P, TT, 6]), sb("mv_e", [P, TT, 2])
        ve, rstd = sb("ve_e", [P, TT]), sb("rstd_e", [P, TT])
        xa = sb("xa", [P, ROWS, TT, C])
        gmax = sb("gmax", [P, T // G])
        perm = sb("perm", [P, CH, T])
        work = sb("work", [P, 2 * TT * C])
        xnT = work[:, 0:CB * T].rearrange("p (cb t) -> p cb t", cb=CB)
        pT = work[:, CB * T:CB * T + 2 * TT * ES].rearrange("p (b t es) -> p b t es", b=2, t=TT)
        spread = work[:].rearrange("p (b s n) -> p b s n", b=SPREAD, s=S_)
        res = work[:].rearrange("p (b g c) -> p b g c", b=2, g=GT)
        big = sb("big", [P, CB * ES * NG])
        perm_x = big[:].rearrange("p (cb es n) -> p cb es n", cb=CB, es=ES)
        res_t = big[:].rearrange("p (n cb es) -> p n cb es", cb=CB, es=ES)
        inner = sb("inner", [P, E_, NG])
        xi = inner[:].rearrange("p e n -> p (e n)").rearrange("p (b t c) -> p b t c", b=ROWS, t=TT)
        ring = sb("ring", [P, 2, OCT * C])
        w1 = ring[:].rearrange("p b (cb es f) -> p b cb es f", cb=CB, es=OCT * S_)
        w2 = ring[:].rearrange("p b (e c) -> p b e c", e=OCT)
        banks = [ctx.enter_context(nc.psum_tensor(f"bank{a}", [P, 512], F32)) for a in range(8)]

        x1_mem = nc.dram_tensor("x1_mem", (SEQS, T, C), F32, kind="Internal").ap()
        NOCT = E_ // OCT
        loaded, chunk_free = sem("loaded"), sem("chunk_free")
        xo_loaded, x1_done, x1_stored = sem("xo_loaded"), sem("x1_done"), sem("x1_stored")
        stats, aggr, var, rs, xn = sem("stats_e"), sem("aggr_e"), sem("var_e"), sem("rs_e"), sem("xn_e")
        trd, xT, lgd, lgs, gm, perm_ok = sem("trd"), sem("xT"), sem("lgd"), sem("lgs"), sem("gm"), sem("perm_ok")
        pTd, pTc = sem("pTd"), sem("pTc")
        gat = sem("gat")
        gat_act, gat_dve = sem("gat_act"), sem("gat_dve")
        w_loaded, w1d, inn = sem("w_loaded"), sem("w1d"), sem("inn")
        zeroed, spread_act, spread_dve = sem("zeroed"), sem("spread_act"), sem("spread_dve")
        w2d, res_act, res_dve = sem("w2d"), sem("res_act"), sem("res_dve")
        rtd, rc, od, fin = sem("rtd"), sem("rc"), sem("od"), sem("fin")
        xr_loaded, stored = sem("xr_loaded"), sem("stored")
        block = ctx.enter_context(nc.Block())

        def dram_rows(mem, n):
            return mem[bass.ds(n, 1)].rearrange("s (t p) c -> p (s t) c", p=P)

        B1 = E_ // 4
        C1 = E_ // 2
        TD = CH * TT

        @block.sync
        def _(sp):
            for dst, src in ((wc, wc_in), (bct, bctie_in), (b1, b1_in), (b2, b2_in)):
                sp.dma_start(dst[:], src).then_inc(loaded, 16)

            def fetch(c, s):
                n = CH * c + s
                if n:
                    sp.wait_ge(xo_loaded, 32 * n)
                sp.dma_start(xa[:, s % ROWS], dram_rows(x_mem, n)).then_inc(xo_loaded, 16)
                sp.dma_start(xi[:, s % ROWS], dram_rows(x_in, n)).then_inc(xo_loaded, 16)

            def fetch_x1(c, s):
                n = CH * c + s
                if n:
                    sp.wait_ge(xr_loaded, 16 * n)
                sp.dma_start(xa[:, s % ROWS], dram_rows(x1_mem, n)).then_inc(xr_loaded, 16)

            def weights(mem, c, k, q):
                if c or k:
                    sp.wait_ge(w_loaded, 16 * (2 * NOCT * c + k))
                sp.dma_start(ring[:, k % 2], mem[q]).then_inc(w_loaded, 16)

            for c in range(CHUNKS):
                if c == 0:
                    for s in range(ROWS):
                        fetch(c, s)
                    weights(w1_in, c, 0, 0)
                    weights(w1_in, c, 1, 1)
                for s in range(CH):
                    n = CH * c + s
                    sp.wait_ge(x1_done, n + 1)
                    if n:
                        sp.wait_ge(x1_stored, 16 * n)
                    sp.dma_start(dram_rows(x1_mem, n), xa[:, s % ROWS]).then_inc(x1_stored, 16)
                    if s + ROWS < CH:
                        sp.wait_ge(gat, 2 * n + 2)
                        sp.wait_ge(x1_stored, 16 * n + 16)
                        fetch(c, s + ROWS)
                sp.wait_ge(xn, CH * c + CH)
                for k in range(2, 2 * NOCT):
                    if k < NOCT + 2:
                        sp.wait_ge(w1d, B1 * c + (k - 1) * (OCT // 4))
                    else:
                        sp.wait_ge(w2d, C1 * c + (k - 1 - NOCT) * (OCT // 2))
                    weights(w1_in if k < NOCT else w2_in, c, k, k % NOCT)
                sp.wait_ge(x1_stored, 16 * (CH * c + CH))
                for s in range(ROWS):
                    fetch_x1(c, s)
                if c + 1 < CHUNKS:
                    sp.wait_ge(w2d, C1 * (c + 1))
                    weights(w1_in, c + 1, 0, 0)
                    weights(w1_in, c + 1, 1, 1)
                for s in range(CH):
                    n = CH * c + s
                    sp.wait_ge(fin, TT * n + TT)
                    if n:
                        sp.wait_ge(stored, 16 * n)
                    sp.dma_start(dram_rows(out, n), xa[:, s % ROWS]).then_inc(stored, 16)
                    if s + ROWS < CH:
                        sp.wait_ge(stored, 16 * n + 16)
                        fetch_x1(c, s + ROWS)
                    elif c + 1 < CHUNKS:
                        sp.wait_ge(stored, 16 * n + 16)
                        fetch(c + 1, s + ROWS - CH)
            sp.wait_ge(stored, 16 * SEQS)

        @block.gpsimd
        def _(pool):
            with pool.Fori(0, SEQS) as n:
                pool.wait_ge(var, n + 1)
                pool.tensor_tensor(rstd[:], ve[:], eps_pow[:], ALU.pow).then_inc(rs, 1)

        @block.tensor
        def _(pe):
            pe.wait_ge(loaded, 64)

            def transpose_norm(c, s):
                n = CH * c + s
                pe.wait_ge(xn, n + 1)
                if s:
                    pe.wait_ge(xT, n)
                for cb in range(CB):
                    for t in range(TT):
                        last = pe.transpose(banks[cb][:, t * P:(t + 1) * P], xi[:, s % ROWS, t, cb * P:(cb + 1) * P], ident[:])
                last.then_inc(trd, 1)

            def logits(c, s):
                n = CH * c + s
                pe.wait_ge(xT, n + 1)
                if s:
                    pe.wait_ge(lgs, n)
                for cb in range(CB):
                    last = pe.matmul(banks[2][:], wc[:, cb, :], xnT[:, cb, :], start=cb == 0, stop=cb == CB - 1)
                last.then_inc(lgd, 1)

            def transpose_perm(c, s):
                n = CH * c + s
                pe.wait_ge(perm_ok, n + 1)
                if s:
                    pe.wait_ge(pTc, n)
                for t in range(TT):
                    last = pe.transpose(banks[3][:, t * P:(t + 1) * P], perm[:, s, t * P:(t + 1) * P], ident[:])
                last.then_inc(pTd, 1)

            def gather(c, s, r):
                k = 2 * s + r
                if r == 0:
                    pe.wait_ge(pTc, CH * c + s + 1)
                if k:
                    pe.wait_ge(gat_act, 2 * CH * c + k)
                    pe.wait_ge(gat_dve, 2 * CH * c + k)
                for t in range(2):
                    for g in range(GT):
                        for cb in range(CB):
                            last = pe.matmul(banks[4 + g][:, (t * CB + cb) * ES:(t * CB + cb + 1) * ES],
                                             xi[G * g:G * g + G, s % ROWS, 2 * r + t, cb * P:(cb + 1) * P],
                                             pT[G * g:G * g + G, s % 2, 2 * r + t, :], start=True, stop=True,
                                             tile_position=(G * g, 0))
                last.then_inc(gat, 1)

            with pe.Fori(0, CHUNKS) as c:
                pe.wait_ge(chunk_free, c + 1)
                transpose_norm(c, 0)
                logits(c, 0)
                transpose_perm(c, 0)
                for s in range(CH):
                    if s + 1 < CH:
                        transpose_norm(c, s + 1)
                    gather(c, s, 0)
                    if s + 1 < CH:
                        logits(c, s + 1)
                    gather(c, s, 1)
                    if s + 1 < CH:
                        transpose_perm(c, s + 1)
                pe.wait_ge(gat_act, 2 * CH * (c + 1))
                pe.wait_ge(gat_dve, 2 * CH * (c + 1))
                for q in range(B1):
                    if q % (OCT // 4) == 0:
                        pe.wait_ge(w_loaded, 16 * (2 * NOCT * c + q // (OCT // 4)) + 16)
                    if q >= 4:
                        pe.wait_ge(inn, E_ * c + 4 * (q - 3))
                    for j in range(4):
                        e = 4 * q + j
                        for cb in range(CB):
                            for s in range(S_):
                                last = pe.matmul(banks[4 + q % 4][EF * s:EF * s + EF, j * NG:(j + 1) * NG],
                                                 w1[:, (e // OCT) % 2, cb, (e % OCT) * S_ + s, :],
                                                 perm_x[:, cb, e * S_ + s, :], start=cb == 0, stop=cb == CB - 1,
                                                 tile_position=(0, EF * s))
                    last.then_inc(w1d, 1)
                for q in range(C1):
                    if q % (OCT // 2) == 0:
                        pe.wait_ge(w_loaded, 16 * (2 * NOCT * c + NOCT + q // (OCT // 2)) + 16)
                    if q >= 2:
                        pe.wait_ge(res_act, C1 * c + q - 1)
                        pe.wait_ge(res_dve, C1 * c + q - 1)
                    for j in range(2):
                        e = 2 * q + j
                        pe.wait_ge(spread_act, E_ * c + e + 1)
                        pe.wait_ge(spread_dve, E_ * c + e + 1)
                        for cb in range(CB):
                            last = pe.matmul(banks[4 * (q % 2) + CB * j + cb][:],
                                             w2[:, (e // OCT) % 2, e % OCT, cb * P:(cb + 1) * P],
                                             spread[:, e % SPREAD].rearrange("p s n -> p (s n)"), start=True, stop=True)
                    last.then_inc(w2d, 1)
                pe.wait_ge(res_act, C1 * (c + 1))
                pe.wait_ge(res_dve, C1 * (c + 1))

                def back(t):
                    if t >= 2:
                        pe.wait_ge(rc, 2 * (TD * c + t - 1))
                    for g in range(GT):
                        for cb in range(CB):
                            last = pe.transpose(banks[2 * (t % 2) + g // 2][:, ((g % 2) * CB + cb) * P:((g % 2) * CB + cb + 1) * P],
                                                res_t[:, GT * t + g, cb, :], ident[:])
                    last.then_inc(rtd, 1)

                back(0)
                for t in range(TD):
                    if t + 1 < TD:
                        back(t + 1)
                    pe.wait_ge(rc, 2 * (TD * c + t) + 2)
                    if t >= 2:
                        pe.wait_ge(fin, TD * c + t - 1)
                    for g in range(GT):
                        last = pe.matmul(banks[4 + t % 2][G * g:G * g + G, 0:C],
                                         perm[:, t // TT, (t % TT) * P + g * G:(t % TT) * P + (g + 1) * G],
                                         res[:, t % 2, g, :], start=True, stop=True, tile_position=(0, G * g))
                    last.then_inc(od, 1)

        @block.scalar
        def _(act):
            with act.Fori(0, CHUNKS) as c:
                act.wait_ge(chunk_free, c + 1)

                def channels(s):
                    n = CH * c + s
                    act.wait_ge(trd, n + 1)
                    if s:
                        act.wait_ge(lgd, n)
                    for cb in range(CB):
                        last = act.activation(xnT[:, cb, :], banks[cb][:], ACT.Identity)
                    last.then_inc(xT, 1)

                def perm_rows(s):
                    act.wait_ge(pTd, CH * c + s + 1)
                    if s >= 2:
                        act.wait_ge(gat, 2 * (CH * c + s) - 2)
                    act.activation(pT[:, s % 2], banks[3][:].rearrange("p (t es) -> p t es", t=TT), ACT.Identity).then_inc(pTc, 1)

                channels(0)
                perm_rows(0)
                for s in range(CH):
                    if s + 1 < CH:
                        channels(s + 1)
                    for r in range(2):
                        act.wait_ge(gat, 2 * (CH * c + s) + r + 1)
                        for g in range(2):
                            n0 = GT * (TT * s + 2 * r) + g
                            last = act.activation(perm_x[:, :, :, n0:n0 + GT + 1:GT].rearrange("p cb es t -> p t cb es"),
                                                  banks[4 + g][:].rearrange("p (t cb es) -> p t cb es", t=2, cb=CB), ACT.Identity)
                        last.then_inc(gat_act, 1)
                    if s + 1 < CH:
                        perm_rows(s + 1)
                act.wait_ge(zeroed, c + 1)

                def spread_low(e):
                    act.wait_ge(inn, E_ * c + e + 1)
                    for s in range(S_ // 2):
                        last = act.activation(spread[EF * s:EF * s + EF, e % SPREAD, s, :], inner[EF * s:EF * s + EF, e, :],
                                              ACT.Identity)
                    last.then_inc(spread_act, 1)

                for e in range(SPREAD):
                    spread_low(e)
                for q in range(C1):
                    act.wait_ge(w2d, C1 * c + q + 1)
                    for e in range(2 * q + SPREAD, min(2 * q + SPREAD + 2, E_)):
                        spread_low(e)
                    for cb in range(CB):
                        last = act.activation(res_t[:, :, cb, 2 * q * S_:(2 * q + 1) * S_].rearrange("p n s -> p s n"),
                                              banks[4 * (q % 2) + cb][:].rearrange("p (s n) -> p s n", s=S_), ACT.Identity)
                    last.then_inc(res_act, 1)

        @block.vector
        def _(dve):
            dve.wait_ge(loaded, 64)
            dve.memset(spare[:], 0.0).then_inc(chunk_free, 1)
            with dve.Fori(0, CHUNKS) as c:
                def norm(s):
                    n = CH * c + s
                    dve.wait_ge(xo_loaded, 32 * n + 32)
                    xs, xw = xa[:, s % ROWS], xi[:, s % ROWS]
                    dve.tensor_tensor(xs, xs, xw, ALU.add).then_inc(x1_done, 1)
                    held(dve, spare[:], x1_done, n + 1)
                    for t in range(TT):
                        last = dve.bn_stats(st[:, t, :], xs[:, t, :])
                    last.then_inc(stats, 1)
                    held(dve, spare[:], stats, n + 1)
                    for t in range(TT):
                        last = dve.bn_aggr(mv[:, t, :], st[:, t, :])
                    last.then_inc(aggr, 1)
                    dve.wait_ge(aggr, n + 1)
                    dve.tensor_scalar(ve[:], mv[:, :, 1], EPS, None, ALU.add).then_inc(var, 1)
                    dve.wait_ge(rs, n + 1)
                    for t in range(TT):
                        last = dve.tensor_scalar(xw[:, t, :], xs[:, t, :], mv[:, t, 0:1], rstd[:, t:t + 1],
                                                 ALU.subtract, ALU.mult)
                    last.then_inc(xn, 1)

                def choose(s):
                    n = CH * c + s
                    dve.wait_ge(lgd, n + 1)
                    l3 = perm[:, s, :].rearrange("p (n t) -> p n t", t=G)
                    dve.scalar_tensor_tensor(l3, banks[2][:].rearrange("p (n t) -> p n t", t=G), bct[:, 0:1],
                                             bct[:, 1:].unsqueeze(1).to_broadcast([P, T // G, G]), ALU.add, ALU.add)\
                       .then_inc(lgs, 1)
                    dve.wait_ge(lgs, n + 1)
                    dve.tensor_reduce(gmax[:], l3, AX.X, ALU.max).then_inc(gm, 1)
                    dve.wait_ge(gm, n + 1)
                    dve.tensor_tensor(l3, l3, gmax[:].unsqueeze(2).to_broadcast([P, T // G, G]), ALU.is_equal).then_inc(perm_ok, 1)

                norm(0)
                choose(0)
                norm(1)
                for s in range(CH):
                    if s + 2 < CH:
                        norm(s + 2)
                    for r in range(2):
                        dve.wait_ge(gat, 2 * (CH * c + s) + r + 1)
                        for g in range(2, GT):
                            n0 = GT * (TT * s + 2 * r) + g
                            last = dve.tensor_copy(perm_x[:, :, :, n0:n0 + GT + 1:GT].rearrange("p cb es t -> p t cb es"),
                                                   banks[4 + g][:].rearrange("p (t cb es) -> p t cb es", t=2, cb=CB))
                        last.then_inc(gat_dve, 1)
                        if r == 0 and s + 1 < CH:
                            choose(s + 1)
                dve.memset(work[:], 0.0).then_inc(zeroed, 1)
                for e in range(E_):
                    if e % 4 == 0:
                        dve.wait_ge(w1d, B1 * c + e // 4 + 1)
                    dve.tensor_scalar(inner[:, e, :], banks[4 + (e // 4) % 4][:, (e % 4) * NG:(e % 4 + 1) * NG],
                                      b1[:, e:e + 1], 0.0, ALU.add, ALU.max).then_inc(inn, 1)
                def spread_high(e):
                    dve.wait_ge(inn, E_ * c + e + 1)
                    for s in range(S_ // 2, S_):
                        last = dve.tensor_copy(spread[EF * s:EF * s + EF, e % SPREAD, s, :], inner[EF * s:EF * s + EF, e, :])
                    last.then_inc(spread_dve, 1)

                for e in range(SPREAD):
                    spread_high(e)
                for q in range(C1):
                    dve.wait_ge(w2d, C1 * c + q + 1)
                    for e in range(2 * q + SPREAD, min(2 * q + SPREAD + 2, E_)):
                        spread_high(e)
                    for cb in range(CB):
                        last = dve.tensor_copy(res_t[:, :, cb, (2 * q + 1) * S_:(2 * q + 2) * S_].rearrange("p n s -> p s n"),
                                               banks[4 * (q % 2) + CB + cb][:].rearrange("p (s n) -> p s n", s=S_))
                    last.then_inc(res_dve, 1)

                def add(t):
                    if t % TT == 0:
                        dve.wait_ge(xr_loaded, 16 * (CH * c + t // TT) + 16)
                    dve.wait_ge(od, TD * c + t + 1)
                    xs = xa[:, (t // TT) % ROWS, t % TT, :]
                    dve.tensor_tensor(xs, xs, banks[4 + t % 2][:, 0:C], ALU.add).then_inc(fin, 1)

                for t in range(TD):
                    dve.wait_ge(rtd, TD * c + t + 1)
                    if t >= 2:
                        dve.wait_ge(od, TD * c + t - 1)
                    for a in range(2):
                        dve.tensor_tensor(res[:, t % 2, 2 * a:2 * a + 2, :],
                                          banks[2 * (t % 2) + a][:].rearrange("p (g c) -> p g c", g=2),
                                          b2[:].unsqueeze(1).to_broadcast([P, 2, C]), ALU.add).then_inc(rc, 1)
                    if t:
                        add(t - 1)
                add(TD - 1)
                dve.wait_ge(fin, TD * (c + 1))
                dve.memset(spare[:], 0.0).then_inc(chunk_free, 1)


def kernel(**inputs):
    import numpy as np
    import concourse.bacc as bacc
    from concourse.bass_utils import run_bass_kernel_spmd

    a = {n: np.asarray(v) for n, v in inputs.items()}
    f = np.float32

    def cols(v):
        return v.reshape(LAYERS, CB, P).transpose(2, 0, 1)

    def rows(v, nb):
        l, o, i = v.shape
        return v.transpose(0, 2, 1).reshape(l, nb, P, o).transpose(0, 2, 1, 3).reshape(l, P, nb * o)

    L0 = {n[8:]: v for n, v in a.items() if n.startswith("L0_attn_")}
    names = ["ln1_w", "ln1_b", "ln2_w", "ln2_b", "time_decay", "time_first", "tmk", "tmv", "tmr", "cmk", "cmr"]
    arrays = {
        "x_in": L0["x"],
        "ln0": np.stack([L0["ln0_w"], L0["ln0_b"]]),
        "par_in": np.stack([cols(L0[n]) for n in names], axis=1),
        "kvr_in": np.concatenate([rows(L0[n], CB) for n in ("Wk", "Wv", "Wr")], axis=2),
        "wo_in": rows(L0["Wo"], CB),
        "wck_in": rows(L0["Wck"], CB),
        "wcr_in": rows(L0["Wcr"], CB),
        "wcv_in": rows(L0["Wcv"], FB),
        "ident_in": np.eye(P, dtype=f),
        "wc_in": a["L0_ffn_Wc"].reshape(CB, P, ES).transpose(1, 0, 2),
        "bctie_in": np.concatenate([a["L0_ffn_bc"].reshape(ES, 1),
                                    np.broadcast_to(np.linspace(0.0, 1e-6, G, dtype=f), (ES, G))], axis=1),
        "w1_in": a["L0_ffn_W1"].reshape(E_ // OCT, OCT * S_, CB, P, EF).transpose(0, 3, 2, 1, 4).reshape(E_ // OCT, P, OCT * C),
        "b1_in": a["L0_ffn_b1"].transpose(1, 2, 0).reshape(S_ * EF, E_),
        "w2_in": a["L0_ffn_W2"].reshape(E_ // OCT, OCT, S_, C, EF).transpose(0, 2, 4, 1, 3).reshape(E_ // OCT, P, OCT * C),
        "b2_in": a["L0_ffn_b2"].reshape(ES, C),
    }
    nc = bacc.Bacc("TRN2", target_bir_lowering=False, num_devices=1)
    args = {}
    for n, v in arrays.items():
        arrays[n] = v = np.ascontiguousarray(v)
        args[n] = nc.dram_tensor(n, v.shape, mybir.dt.from_np(v.dtype), kind="ExternalInput").ap()
    args["out"] = nc.dram_tensor("out", (SEQS, T, C), F32, kind="ExternalOutput").ap()
    rwkv_moe(nc, **args)
    r = run_bass_kernel_spmd(nc, [arrays], core_ids=[0])
    return r.results[0]["out"]
```
